# Optimizing a Trainium2 kernel written in Bass

```python
import numpy as np
import jax
import jax.numpy as jnp

def _softmax(x, axis=-1):
    return jax.nn.softmax(x, axis=axis)

def _gelu(x):
    return jax.nn.gelu(x, approximate=True)

def _silu(x):
    return jax.nn.silu(x)

def _sigmoid(x):
    return jax.nn.sigmoid(x)

def _layernorm(x, axis=-1, eps=1e-05):
    m = jnp.mean(x, axis=axis, keepdims=True)
    v = jnp.var(x, axis=axis, keepdims=True)
    return (x - m) / jnp.sqrt(v + eps)

def _scatter_add(tgt, idx, src, axis=0):
    return tgt.at[idx].add(src)

def _segment_sum(src, seg, n):
    return jax.ops.segment_sum(src, seg, n)
kernel_name = 'mk_gnn_resnorm_d1_gnn_r8_0c96a6'

def setup_inputs(seed: int=0):
    np.random.seed(seed)
    _w = jnp.asarray

    def _rec_inputs():
        import jax
        import jax.numpy as jnp
        _gk = jax.random.key(seed)
        x = -0.0006008 + 1.001 * jax.random.normal(jax.random.fold_in(_gk, 1), (6250, 128), jnp.float32)
        src = jax.random.randint(jax.random.fold_in(_gk, 2), (200000,), 0, 6250, jnp.int32)
        dst = jax.random.randint(jax.random.fold_in(_gk, 3), (200000,), 0, 6250, jnp.int32)
        _o = jnp.argsort(dst, stable=True)
        src = src[_o]
        dst = dst[_o]
        edge_type_65 = jax.random.randint(jax.random.fold_in(_gk, 12), (200000,), 0, 65, jnp.int32)
        return (x, src, dst, edge_type_65)
    x, src, dst, edge_type_65 = _rec_inputs()

    def _L0_gnn_setup():
        import jax, jax.numpy as jnp
        import numpy as np
        EPS = 1e-05
        key = jax.random.key(seed)
        ks = jax.random.split(key, 10)
        N, E, F_IN, F_OUT, R = (2500, 80000, 128, 128, 65)
        x = jax.random.normal(ks[0], (N, F_IN), dtype=jnp.float32)
        edge_index = jax.random.randint(ks[1], (2, E), 0, N, dtype=jnp.int64)
        edge_type = jax.random.randint(ks[2], (E,), 0, R, dtype=jnp.int64)
        s = 1.0 / np.sqrt(F_IN)
        W_rel = jax.random.normal(ks[3], (R, F_IN, F_OUT), dtype=jnp.float32) * s
        W_root = jax.random.normal(ks[4], (F_IN, F_OUT), dtype=jnp.float32) * s
        bias = jax.random.normal(ks[5], (F_OUT,), dtype=jnp.float32) * s
        W_res = jax.random.normal(ks[6], (F_IN, F_OUT), dtype=jnp.float32) * s
        b_res = jax.random.normal(ks[7], (F_OUT,), dtype=jnp.float32) * s
        gamma = jnp.ones((F_OUT,), dtype=jnp.float32)
        beta = jnp.zeros((F_OUT,), dtype=jnp.float32)
        return {'x': x, 'edge_index': edge_index, 'edge_type': edge_type, 'W_rel': W_rel, 'W_root': W_root, 'bias': bias, 'W_res': W_res, 'b_res': b_res, 'gamma': gamma, 'beta': beta}
    _L0_gnn_all = _L0_gnn_setup()
    _L0_gnn_in = {k: v for k, v in _L0_gnn_all.items() if k in ('W_rel', 'W_root', 'bias', 'W_res', 'b_res', 'gamma', 'beta')}
    del _L0_gnn_all
    return {'x': x, 'src': src, 'dst': dst, 'edge_type_65': edge_type_65, 'L0_gnn_W_rel': _L0_gnn_in['W_rel'], 'L0_gnn_W_root': _L0_gnn_in['W_root'], 'L0_gnn_bias': _L0_gnn_in['bias'], 'L0_gnn_W_res': _L0_gnn_in['W_res'], 'L0_gnn_b_res': _L0_gnn_in['b_res'], 'L0_gnn_gamma': _L0_gnn_in['gamma'], 'L0_gnn_beta': _L0_gnn_in['beta']}

def reference(x, src, dst, edge_type_65, L0_gnn_W_rel, L0_gnn_W_root, L0_gnn_bias, L0_gnn_W_res, L0_gnn_b_res, L0_gnn_gamma, L0_gnn_beta):
    import jax
    import jax.numpy as jnp

    def _L0_gnn_ref(x, edge_index, edge_type, W_rel, W_root, bias, W_res, b_res, gamma, beta):
        import jax, jax.numpy as jnp
        import numpy as np
        EPS = 1e-05
        N, F_in = x.shape
        R = W_rel.shape[0]
        src, dst = (edge_index[0], edge_index[1])
        seg = dst * R + edge_type
        msrc = x[src]
        sums = jax.ops.segment_sum(msrc, seg, num_segments=N * R).reshape(N, R, F_in)
        cnt = jax.ops.segment_sum(jnp.ones_like(seg, dtype=x.dtype), seg, num_segments=N * R).reshape(N, R, 1)
        agg = sums / jnp.maximum(cnt, 1.0)
        conv = jnp.einsum('nri,rio->no', agg, W_rel) + x @ W_root + bias
        h = conv + x @ W_res + b_res
        mean = h.mean(axis=0)
        var = jnp.mean(jnp.square(h - mean), axis=0)
        h = (h - mean) * jax.lax.rsqrt(var + EPS) * gamma + beta
        return jax.nn.relu(h)
    edge_index = jnp.stack([src, dst])
    x = _layernorm(x + _L0_gnn_ref(x, edge_index, edge_type_65, L0_gnn_W_rel, L0_gnn_W_root, L0_gnn_bias, L0_gnn_W_res, L0_gnn_b_res, L0_gnn_gamma, L0_gnn_beta), axis=-1)
    return x

_drawn_inputs = setup_inputs


def setup_inputs(seed=0):
    import zlib

    import numpy as np

    out = dict(_drawn_inputs(seed))
    spreads = {'L0_gnn_gamma': (1.0, 0.2), 'L0_gnn_beta': (0.0, 0.1)}
    factors = {}
    for name, (base, spread) in spreads.items():
        noise = np.random.default_rng([zlib.crc32(name.encode()), seed]).standard_normal(out[name].shape)
        drawn = base * np.exp(spread * noise) if base else spread * noise
        out[name] = jnp.asarray(drawn.astype(out[name].dtype))
    for name, factor in factors.items():
        out[name] = (out[name] * factor).astype(out[name].dtype)
    return out
```

```python
from contextlib import ExitStack

import concourse.bass as bass
from concourse import mybir
import numpy as np

F32 = mybir.dt.float32
BF16 = mybir.dt.bfloat16
I32 = mybir.dt.int32
ALU = mybir.AluOpType
ACT = mybir.ActivationFunctionType
AX = mybir.AxisListType

P = 128
CH = 16
WIN = 80
GE = P * CH
RPM = 4
EPS = 1e-5


def ceil_div(a, b):
    return -(-a // b)


def gnn(nc, x, src, dst, et, w_rel, w_root, bias, w_res, b_res, gamma, beta, out):
    N, F = x.shape
    E = src.shape[0]
    R = w_rel.shape[0]
    assert F == P and w_rel.shape[1] == P and w_rel.shape[2] == P
    NT = ceil_div(N, P)
    NLAST = N - (NT - 1) * P
    G = ceil_div(E, GE)
    ELAST = E - (G - 1) * GE
    PLAST = ELAST // CH
    assert ELAST % CH == 0 and G % 2 == 0 and NT % 2 == 1 and G == 2 * NT
    PASSES = ceil_div(N, WIN)
    NPIECE = R // RPM
    assert R == NPIECE * RPM + 1 and NPIECE % 4 == 0
    HC = N + WIN
    assert HC >= NT * P
    BG = 7
    NB = NT // BG
    assert NB * BG == NT and NB >= 2
    BNC = 250
    assert N % BNC == 0

    ytab = nc.dram_tensor("ytab", (NT * P * R, F), F32, kind="Internal").ap()
    etpad = nc.dram_tensor("etpad", (G * GE,), BF16, kind="Internal").ap()
    ytab_tiles = ytab.rearrange("(t p r) f -> t p (r f)", p=P, r=R)
    etpad_rows = etpad.rearrange("(g e) -> g e", e=GE)

    with ExitStack() as ctx:
        def sb(name, shape, dt):
            return ctx.enter_context(nc.sbuf_tensor(name, shape, dt))

        def pb(name, shape, dt):
            return ctx.enter_context(nc.psum_tensor(name, shape, dt))

        def sem(name):
            return ctx.enter_context(nc.semaphore(name))

        wall = sb("wall", [P, R * F], F32)
        stage = sb("stage", [P, 2, R * F], F32)
        H = sb("H", [P, HC], F32)
        CT = sb("CT", [R, HC], F32)
        srcs = sb("srcs", [P, G * CH], I32)
        dsts = sb("dsts", [P, G * CH], I32)
        ets = sb("ets", [P, G * CH], I32)
        et16 = sb("et16", [P, G * CH], BF16)
        drow = sb("drow", [1, G], F32)
        basec = sb("basec", [P, G], F32)
        passb = sb("passb", [P, PASSES], F32)
        dloc2 = sb("dloc2", [P, 2, CH], F32)
        onehot_n = sb("onehot_n", [P, CH, WIN], BF16)
        onehot_r = sb("onehot_r", [P, CH, R], BF16)
        idx = [sb(f"idx{s}", [P, CH], I32) for s in range(2)]
        etb = sb("etb", [R, 2, GE], BF16)
        rel1h = sb("rel1h", [R, 2, GE], BF16)
        wts = sb("wts", [P, 2, CH, WIN], F32)
        cf = sb("cf", [R, 4, WIN], F32)
        cinv = sb("cinv", [R, 2, 3, WIN], BF16)
        xt_in = sb("xt_in", [P, 2, F], F32)
        xT = [sb(f"xT{s}", [P, P], F32) for s in range(2)]
        wroot = sb("wroot", [P, F], F32)
        wres = sb("wres", [P, F], F32)
        ident = sb("ident", [P, P], F32)
        ones = sb("ones", [P, P], F32)
        iota_n = sb("iota_n", [P, WIN], F32)
        iota_r = sb("iota_r", [P, R], F32)
        pidx = sb("pidx", [P, 1], F32)
        cols = sb("cols", [P, 16], F32)
        flag = sb("flag", [1, 1], I32)
        bst = sb("bst", [P, N // BNC, 6], F32)
        ys = [stage[:, s, 0:CH * F].rearrange("p (k f) -> p k f", f=F) for s in range(2)]
        xin = [stage[:, s, 2 * BG * F:3 * BG * F].rearrange("p (t f) -> p t f", f=F) for s in range(2)]
        zo = [stage[:, s, 3 * BG * F:4 * BG * F].rearrange("p (t f) -> p t f", f=F) for s in range(2)]
        oo = [stage[:, s, 4 * BG * F:5 * BG * F].rearrange("p (t f) -> p t f", f=F) for s in range(2)]
        lst = [stage[:, s, 6 * BG * F:6 * BG * F + BG * 6].rearrange("p (t c) -> p t c", c=6) for s in range(2)]
        lmv = [stage[:, s, 6 * BG * F + 64:6 * BG * F + 64 + BG * 2].rearrange("p (t c) -> p t c", c=2)
               for s in range(2)]
        lrs = [stage[:, s, 6 * BG * F + 96:6 * BG * F + 96 + 3 * BG].rearrange("p (c t) -> p c t", c=3)
               for s in range(2)]
        B_BIAS, B_RES, GAM, BET, BSUM, MX, MN, BAD, MV, STD, SCL, SHF = 0, 1, 2, 3, 4, 5, 6, 7, 8, 10, 11, 12

        bank = [pb(f"bank{i}", [P, 512], F32) for i in range(4)]
        root_ps = pb("root_ps", [P, 512], F32)
        tr_ps = pb("tr_ps", [P, 512], F32)
        acc_ps = [pb(f"acc_ps{i}", [P, 512], F32) for i in range(2)]

        loaded = {n: sem("loaded_" + n) for n in ("src", "dst", "et", "wrel", "small")}
        padded = sem("padded")
        pads_in = sem("pads_in")
        consts = sem("consts")
        et16_done = sem("et16_done")
        etpad_in_dram = sem("etpad_in_dram")
        base_row = sem("base_row")
        base_ps = sem("base_ps")
        bad_rdy = sem("bad_rdy")
        bad_ps = sem("bad_ps")
        flag_rdy = sem("flag_rdy")
        dve_step = sem("dve_step")
        x_in = [sem(f"x_in{s}") for s in range(2)]
        xT_ps = sem("xT_ps")
        xT_rdy = sem("xT_rdy")
        piece_ps = sem("piece_ps")
        piece_out = sem("piece_out")
        root_done = sem("root_done")
        root_out = sem("root_out")
        tab_out = [sem(f"tab_out{s}") for s in range(2)]
        oh_rdy = sem("oh_rdy")
        cnt_ps = sem("cnt_ps")
        cnt_add = sem("cnt_add")
        cnt_step = sem("cnt_step")
        etb_in = [sem(f"etb_in{s}") for s in range(2)]
        idx_rdy = sem("idx_rdy")
        prep_step = sem("prep_step")
        rel_rdy = sem("rel_rdy")
        look_ps = sem("look_ps")
        wts_rdy = sem("wts_rdy")
        pool_turn = sem("pool_turn")
        sp_turn = sem("sp_turn")
        gathered = [sem(f"gathered{s}") for s in range(2)]
        msg_ps = sem("msg_ps")
        msg_add = sem("msg_add")
        norm_rdy = sem("norm_rdy")
        std_rdy = sem("std_rdy")
        relu_rdy = sem("relu_rdy")
        tr_done = sem("tr_done")
        z_add = sem("z_add")
        fin_step = sem("fin_step")
        lv_rdy = sem("lv_rdy")
        lstd_rdy = sem("lstd_rdy")
        o_rdy = sem("o_rdy")
        xr_in = [sem(f"xr_in{s}") for s in range(2)]
        o_out = [sem(f"o_out{s}") for s in range(2)]

        block = ctx.enter_context(nc.Block())
        NC_SMALL = 7

        def col(c, n=1):
            return cols[:, c:c + n]

        def colvec(v):
            return v.rearrange("(p a) -> p a", a=1)

        def grp(t, g):
            return t[:, bass.ds(g * CH, CH)]

        def both_paths(eng, fast, general):
            eng.wait_ge(flag_rdy, 1)
            bad = eng.value_load(flag[0:1, 0:1], min_val=0, max_val=P)
            with eng.If(bad == 0):
                fast()
            with eng.Else():
                general()

        def general_passes(eng, one_pass, before_pass):
            with eng.Fori(0, PASSES) as p:
                one_pass(p)
                before_pass(p)

        @block.sync
        def _(sp):
            for n, t, v in (("dst", dsts, dst), ("et", ets, et), ("src", srcs, src)):
                full = v[0:(G - 1) * GE].rearrange("(g p k) -> p g k", p=P, k=CH)
                sp.dma_start(t[:, 0:(G - 1) * CH].rearrange("p (g k) -> p g k", k=CH), full).then_inc(loaded[n], 16)
                sp.wait_ge(padded, 2)
                sp.dma_start(t[0:PLAST, (G - 1) * CH:G * CH],
                             v[(G - 1) * GE:E].rearrange("(p k) -> p k", k=CH)).then_inc(loaded[n], 16)

            def load_x(i, s):
                sp.dma_start(xt_in[:, s, :], x[bass.ds(i * P, P), :]).then_inc(x_in[s], 16)

            load_x(0, 0)
            sp.dma_start(wroot[:], w_root).then_inc(loaded["small"], 16)
            sp.dma_start(wres[:], w_res).then_inc(loaded["small"], 16)
            for c, v in ((B_BIAS, bias), (B_RES, b_res), (GAM, gamma), (BET, beta)):
                sp.dma_start(col(c), colvec(v)).then_inc(loaded["small"], 16)
            sp.dma_start(wall[:].rearrange("p (r f) -> p r f", f=F),
                         w_rel.rearrange("r p f -> p r f")).then_inc(loaded["wrel"], 16)
            sp.wait_ge(et16_done, 1)
            sp.dma_start(etpad.rearrange("(g p k) -> p g k", p=P, k=CH),
                         et16[:].rearrange("p (g k) -> p g k", k=CH)).then_inc(etpad_in_dram, 16)
            load_x(1, 1)

            def store_tile(i, s):
                sp.wait_ge(piece_out, (i + 1) * NPIECE)
                sp.wait_ge(root_out, i + 1)
                sp.sem_inc(sp_turn)
                sp.dma_start(ytab_tiles[bass.ds(i, 1), :, :].rearrange("t p c -> (t p) c"), stage[:, s, :]).then_inc(tab_out[s], 16)

            with sp.Fori(0, (NT - 3) // 2) as j:
                for s in range(2):
                    i = 2 * j + s
                    sp.wait_ge(xT_ps, i + 1)
                    sp.sem_inc(sp_turn)
                    load_x(i + 2, s)
                    store_tile(i, s)
            for i in range(NT - 3, NT):
                if i + 2 < NT - 1:
                    sp.wait_ge(xT_ps, i + 1)
                    load_x(i + 2, i % 2)
                elif i + 2 == NT - 1:
                    sp.wait_ge(xT_ps, i + 1)
                    sp.wait_ge(padded, 3)
                    sp.dma_start(xt_in[0:NLAST, i % 2, :], x[i * P + 2 * P:N, :]).then_inc(x_in[i % 2], 16)
                store_tile(i, i % 2)

            sp.wait_ge(etpad_in_dram, 16)

            def load_etb(p, g, s, first):
                if not first:
                    sp.wait_ge(rel_rdy, p * G + g - 1)
                    sp.sem_inc(sp_turn)
                sp.dma_start(etb[:, s, :], etpad_rows[bass.ds(g, 1), :].to_broadcast([R, GE])).then_inc(etb_in[s], 16)

            def etb_pass(p):
                for s in range(2):
                    load_etb(p, s, s, True)
                with sp.Fori(1, G // 2) as j:
                    for s in range(2):
                        load_etb(p, 2 * j + s, s, False)

            def general_after(p):
                sp.wait_ge(msg_add, (p + 1) * G)
                sp.sem_inc(sp_turn)

            both_paths(sp, lambda: etb_pass(0), lambda: general_passes(sp, etb_pass, general_after))

            def rows(t, b, n):
                return t[bass.ds(b * BG * P, n * P), :].rearrange("(t p) f -> p t f", p=P)

            def load_res(b, s):
                if isinstance(b, int) and b == NB - 1:
                    sp.dma_start(xin[s][:, 0:BG - 1, :], rows(x, b, BG - 1)).then_inc(xr_in[s], 16)
                    sp.dma_start(xin[s][0:NLAST, BG - 1, :], x[(NT - 1) * P:N, :]).then_inc(xr_in[s], 16)
                else:
                    sp.dma_start(xin[s], rows(x, b, BG)).then_inc(xr_in[s], 16)

            sp.wait_ge(norm_rdy, 1)
            load_res(0, 0)
            load_res(1, 1)
            for b in range(NB):
                s = b % 2
                sp.wait_ge(o_rdy, b + 1)
                if b < NB - 1:
                    sp.dma_start(rows(out, b, BG), oo[s]).then_inc(o_out[s], 16)
                    if b + 2 < NB:
                        load_res(b + 2, s)
                else:
                    sp.dma_start(rows(out, b, BG - 1), oo[s][:, 0:BG - 1, :]).then_inc(o_out[s], 16)
                    sp.dma_start(out[(NT - 1) * P:N, :], oo[s][0:NLAST, BG - 1, :]).then_inc(o_out[s], 16)
            sp.wait_ge(o_out[(NB - 1) % 2], 16 * ((NB + 1) // 2 + 1))
            sp.wait_ge(o_out[NB % 2], 16 * (NB // 2))

        @block.gpsimd
        def _(pool):
            nc.gpsimd.memset(ets[:, (G - 1) * CH:G * CH], -1).then_inc(padded, 1)
            nc.gpsimd.memset(srcs[:, (G - 1) * CH:G * CH], 1).then_inc(padded, 1)
            pool.dma_start(dsts[PLAST:P, (G - 1) * CH:G * CH],
                           dst[E - CH:E].rearrange("(a k) -> a k", a=1).to_broadcast([P - PLAST, CH])).then_inc(pads_in, 16)
            nc.gpsimd.memset(ones[:], 1.0).then_inc(consts, 1)
            pool.wait_ge(consts, 1)
            nc.gpsimd.affine_select(out=ident[:], in_=ones[:], compare_op=ALU.is_equal, fill=0.0, base=0,
                                    pattern=[[-1, P]], channel_multiplier=1).then_inc(consts, 1)
            nc.gpsimd.iota(iota_n[:], [[1, WIN]], base=0, channel_multiplier=0,
                           allow_small_or_imprecise_dtypes=True).then_inc(consts, 1)
            nc.gpsimd.iota(iota_r[:], [[1, R]], base=0, channel_multiplier=0,
                           allow_small_or_imprecise_dtypes=True).then_inc(consts, 1)
            nc.gpsimd.iota(pidx[:], [[1, 1]], base=0, channel_multiplier=1,
                           allow_small_or_imprecise_dtypes=True).then_inc(consts, 1)
            nc.gpsimd.iota(passb[:], [[WIN, PASSES]], base=0, channel_multiplier=0,
                           allow_small_or_imprecise_dtypes=True).then_inc(consts, 1)
            nc.gpsimd.memset(CT[:], 0.0).then_inc(consts, 1)
            nc.gpsimd.memset(H[:, NT * P:HC], 0.0).then_inc(consts, 1)
            pool.wait_ge(xT_ps, NT - 2)
            nc.gpsimd.memset(xt_in[:, (NT - 1) % 2, :], 0.0).then_inc(padded, 1)

            for s in range(2):
                pool.wait_ge(tab_out[s], 16 * ((NT + 1 - s) // 2))

            def gather(p, g, s, first):
                pool.wait_ge(idx_rdy, p * G + g + 1)
                if not first:
                    pool.wait_ge(msg_ps, p * G + g - 1)
                pool.sem_inc(pool_turn)
                for k in range(CH):
                    pool.indirect_dma_start(
                        out=ys[s][:, k, :], out_offset=None, in_=ytab,
                        in_offset=bass.IndirectOffsetOnAxis(ap=idx[s][:, k:k + 1], axis=0)).then_inc(gathered[s], 16)

            def gather_pass(p):
                for s in range(2):
                    gather(p, s, s, True)
                with pool.Fori(1, G // 2) as j:
                    for s in range(2):
                        gather(p, 2 * j + s, s, False)

            def general_after(p):
                pool.wait_ge(msg_add, (p + 1) * G)
                pool.sem_inc(pool_turn)

            both_paths(pool, lambda: gather_pass(0), lambda: general_passes(pool, gather_pass, general_after))

        @block.tensor
        def _(pe):
            pe.wait_ge(base_row, 1)
            pe.wait_ge(consts, 2)
            nc.tensor.matmul(tr_ps[:, 256:256 + G], ones[0:1, :], drow[:], start=True, stop=True).then_inc(base_ps, 1)
            pe.wait_ge(bad_rdy, 1)
            nc.tensor.matmul(tr_ps[0:1, 384:385], col(BAD), ones[:, 0:1], start=True, stop=True).then_inc(bad_ps, 1)
            pe.wait_ge(flag_rdy, 1)

            def transpose_x(i, s, first, last):
                pe.wait_ge(x_in[s], 8 * (i - s) + 16)
                if not first:
                    pe.wait_ge(xT_rdy, i)
                nc.tensor.transpose(tr_ps[:, 0:P], xt_in[:, s, :], ident[:]).then_inc(xT_ps, 1)

            def table_tile(i, s, first, last):
                if not last:
                    transpose_x(i + 1, 1 - s, False, False)
                pe.wait_ge(xT_rdy, i + 1)
                for q in range(NPIECE):
                    if not (first and q < 4):
                        pe.wait_ge(piece_out, i * NPIECE + q - 3)
                    nc.tensor.matmul(bank[q % 4][:], xT[s][:], wall[:, q * 512:(q + 1) * 512],
                                     start=True, stop=True).then_inc(piece_ps, 1)
                    if q == 7:
                        if not first:
                            pe.wait_ge(root_out, i)
                        nc.tensor.matmul(root_ps[:, P:2 * P], xT[s][:], wall[:, NPIECE * 512:],
                                         start=True, stop=True)
                        nc.tensor.matmul(root_ps[:, 0:P], wroot[:], xT[s][:], start=True, stop=False)
                        nc.tensor.matmul(root_ps[:, 0:P], wres[:], xT[s][:], start=False,
                                         stop=True).then_inc(root_done, 1)

            def count_group(p, g, first):
                pe.wait_ge(oh_rdy, p * G + g + 1)
                if not first:
                    pe.wait_ge(cnt_add, p * G + g)
                for k in range(CH):
                    ins = nc.tensor.matmul(acc_ps[0][0:R, 0:WIN], onehot_r[:, k, :], onehot_n[:, k, :],
                                           start=(k == 0), stop=(k == CH - 1))
                ins.then_inc(cnt_ps, 1)

            pe.wait_ge(loaded["small"], 16 * (NC_SMALL - 1))
            pe.wait_ge(loaded["wrel"], 16)
            transpose_x(0, 0, True, False)

            def table_and_counts():
                table_tile(0, 0, True, False)
                count_group(0, 0, True)
                count_group(0, 1, False)
                with pe.Fori(0, (NT - 3) // 2) as j:
                    for u in (1, 2):
                        i = 2 * j + u
                        table_tile(i, u % 2, False, False)
                        count_group(0, 2 * i, False)
                        count_group(0, 2 * i + 1, False)
                for i in (NT - 2, NT - 1):
                    table_tile(i, i % 2, False, i == NT - 1)
                    count_group(0, 2 * i, False)
                    count_group(0, 2 * i + 1, False)

            def count_pass(p):
                count_group(p, 0, True)
                with pe.Fori(1, G) as g:
                    count_group(p, g, False)

            def count_after(p):
                pe.wait_ge(cnt_add, (p + 1) * G)

            def table_then_counts():
                table_tile(0, 0, True, False)
                with pe.Fori(0, (NT - 3) // 2) as j:
                    for u in (1, 2):
                        table_tile(2 * j + u, u % 2, False, False)
                for i in (NT - 2, NT - 1):
                    table_tile(i, i % 2, False, i == NT - 1)
                general_passes(pe, count_pass, count_after)

            def lookup(p, g, s, first):
                pe.wait_ge(rel_rdy, p * G + g + 1)
                rel = rel1h[:, s, :].rearrange("r (p k) -> r k p", k=CH)
                for b in range(4):
                    if not first:
                        pe.wait_ge(wts_rdy, (p * G + g - 1) * CH + 4 * b + 4)
                    for k in range(4 * b, 4 * b + 4):
                        for part in range(3):
                            ins = nc.tensor.matmul(bank[b][:, (k - 4 * b) * WIN:(k - 4 * b + 1) * WIN],
                                                   rel[:, k, :], cinv[:, s, part, :],
                                                   start=(part == 0), stop=(part == 2))
                    ins.then_inc(look_ps, 1)

            def messages(p, g, s, first2):
                pe.wait_ge(gathered[s], (p * (G // 2) + (g - s) // 2 + 1) * 16 * CH if not isinstance(g, int)
                           else p * (G // 2) * 16 * CH + (g // 2 + 1) * 16 * CH)
                if not first2:
                    pe.wait_ge(msg_add, p * G + g - 1)
                for k in range(CH):
                    pe.wait_ge(wts_rdy, (p * G + g) * CH + k + 1)
                    ins = nc.tensor.matmul(acc_ps[s][:, 0:WIN], ys[s][:, k, :], wts[:, s, k, :],
                                           start=(k == 0), stop=(k == CH - 1))
                ins.then_inc(msg_ps, 1)

            def message_pass(p):
                for g in range(2):
                    lookup(p, g, g, g == 0)
                    messages(p, g, g, True)
                with pe.Fori(1, G // 2) as j:
                    for s in range(2):
                        lookup(p, 2 * j + s, s, False)
                        messages(p, 2 * j + s, s, False)

            def general_after(p):
                pe.wait_ge(msg_add, (p + 1) * G)

            def fast():
                table_and_counts()
                pe.wait_ge(piece_out, NT * NPIECE)
                message_pass(0)

            def general():
                table_then_counts()
                pe.wait_ge(piece_out, NT * NPIECE)
                general_passes(pe, message_pass, general_after)

            both_paths(pe, fast, general)

            for b in range(NB):
                pe.wait_ge(relu_rdy, b + 1)
                for t in range(BG):
                    i = b * BG + t
                    if i >= 4:
                        pe.wait_ge(z_add, i - 3)
                    nc.tensor.transpose(bank[i % 4][:, 0:P], H[:, i * P:(i + 1) * P],
                                        ident[:]).then_inc(tr_done, 1)

        @block.scalar
        def _(act):
            def tile(i, s, first2):
                act.wait_ge(xT_ps, i + 1)
                nc.scalar.activation(xT[s][:], tr_ps[:, 0:P], ACT.Copy).then_inc(xT_rdy, 1)
                if not first2:
                    act.wait_ge(tab_out[s], 8 * (i - s))
                for q in range(NPIECE):
                    act.wait_ge(piece_ps, i * NPIECE + q + 1)
                    nc.scalar.activation(stage[:, s, q * 512:(q + 1) * 512], bank[q % 4][:],
                                         ACT.Copy).then_inc(piece_out, 1)
                act.wait_ge(root_done, i + 1)
                nc.scalar.activation(H[:, bass.ds(i * P, P)], root_ps[:, 0:P], ACT.Identity, bias=col(BSUM))
                nc.scalar.activation(stage[:, s, NPIECE * 512:], root_ps[:, P:2 * P],
                                     ACT.Copy).then_inc(root_out, 1)

            act.wait_ge(base_ps, 1)
            act.wait_ge(dve_step, 2)
            tile(0, 0, True)
            tile(1, 1, True)
            with act.Fori(1, NT // 2) as j:
                for s in range(2):
                    tile(2 * j + s, s, False)
            tile(NT - 1, 0, False)

            act.wait_ge(norm_rdy, 1)
            nc.scalar.activation(col(STD), col(STD), ACT.Sqrt).then_inc(std_rdy, 1)
            act.wait_ge(norm_rdy, 2)
            for b in range(NB):
                h = H[:, b * BG * P:(b + 1) * BG * P]
                nc.scalar.activation(h, h, ACT.Relu, bias=col(SHF), scale=col(SCL)).then_inc(relu_rdy, 1)
                if b >= 1:
                    act.wait_ge(lv_rdy, b)
                    nc.scalar.activation(lrs[(b - 1) % 2][:, 1, :], lrs[(b - 1) % 2][:, 0, :],
                                         ACT.Sqrt).then_inc(lstd_rdy, 1)
            act.wait_ge(lv_rdy, NB)
            nc.scalar.activation(lrs[(NB - 1) % 2][:, 1, :], lrs[(NB - 1) % 2][:, 0, :],
                                 ACT.Sqrt).then_inc(lstd_rdy, 1)

        @block.vector
        def _(dve):
            dve.wait_ge(loaded["small"], 16 * (NC_SMALL - 1))
            nc.vector.tensor_tensor(col(BSUM), col(B_BIAS), col(B_RES), ALU.add).then_inc(dve_step, 1)
            dve.wait_ge(loaded["dst"], 32)
            dve.wait_ge(pads_in, 16)
            nc.vector.tensor_copy(drow[:], dsts[0:1, :].rearrange("p (g k) -> p g k", k=CH)[:, :, 0]
                                  ).then_inc(base_row, 1)
            dve.wait_ge(base_ps, 1)
            nc.vector.tensor_copy(basec[:], tr_ps[:, 256:256 + G]).then_inc(dve_step, 1)
            dve.wait_ge(dve_step, 2)
            local = stage[:, 0, 0:G * CH].rearrange("p (g k) -> p g k", k=CH)
            nc.vector.tensor_tensor(local, dsts[:].rearrange("p (g k) -> p g k", k=CH),
                                    basec[:].rearrange("p (g a) -> p g a", a=1).to_broadcast([P, G, CH]),
                                    ALU.subtract).then_inc(dve_step, 1)
            dve.wait_ge(dve_step, 3)
            nc.vector.tensor_reduce(col(MX), stage[:, 0, 0:G * CH], AX.X, ALU.max).then_inc(dve_step, 1)
            nc.vector.tensor_reduce(col(MN), stage[:, 0, 0:G * CH], AX.X, ALU.min).then_inc(dve_step, 1)
            dve.wait_ge(dve_step, 5)
            nc.vector.tensor_scalar(col(MX), col(MX), float(WIN - 1), None, ALU.is_gt).then_inc(dve_step, 1)
            dve.wait_ge(dve_step, 6)
            nc.vector.scalar_tensor_tensor(out=col(BAD), in0=col(MN), scalar=0.0, in1=col(MX), op0=ALU.is_lt,
                                           op1=ALU.max).then_inc(bad_rdy, 1)
            dve.wait_ge(bad_ps, 1)
            nc.vector.tensor_copy(flag[:], tr_ps[0:1, 384:385]).then_inc(flag_rdy, 1)
            dve.wait_ge(loaded["et"], 32)
            dve.wait_ge(loaded["src"], 32)
            nc.vector.tensor_copy(et16[:], ets[:]).then_inc(et16_done, 1)
            dve.wait_ge(consts, 8)

            def bcast_k(t2, n):
                return t2.rearrange("p (k a) -> p k a", a=1).to_broadcast([t2.shape[0], CH, n])

            def bcast_n(t2, n):
                return t2.rearrange("p (a n) -> p a n", a=1).to_broadcast([t2.shape[0], CH, n])

            def local_dst(g, slot, base_col):
                return nc.vector.tensor_tensor(dloc2[:, slot, :], grp(dsts, g), base_col.to_broadcast([P, CH]),
                                               ALU.subtract)

            def count_build(p, g, base_col, first):
                if not first:
                    dve.wait_ge(cnt_ps, p * G + g)
                local_dst(g, 0, base_col).then_inc(cnt_step, 1)
                nc.vector.tensor_tensor(onehot_r[:], bcast_n(iota_r[:], R), bcast_k(grp(ets, g), R),
                                        ALU.is_equal).then_inc(cnt_step, 1)
                dve.wait_ge(cnt_step, (p * G + g) * 2 + 2)
                nc.vector.tensor_tensor(onehot_n[:], bcast_n(iota_n[:], WIN), bcast_k(dloc2[:, 0, :], WIN),
                                        ALU.is_equal).then_inc(oh_rdy, 1)

            def count_sum(p, g, base):
                dve.wait_ge(cnt_ps, p * G + g + 1)
                w = CT[:, bass.ds(base, WIN)]
                nc.vector.tensor_tensor(w, w, acc_ps[0][0:R, 0:WIN], ALU.add).then_inc(cnt_add, 1)

            def fast_base(g):
                return dve.value_load(dsts[0:1, bass.ds(g * CH, 1)], min_val=0, max_val=N - 1)

            def fast_col(g):
                return basec[:, bass.ds(g, 1)]

            def count_one(p, g, base_of, col_of, first):
                base = base_of(g)
                if not first:
                    dve.wait_ge(cnt_add, p * G + g)
                count_build(p, g, col_of(g), first)
                count_sum(p, g, base)

            def count_pass(p, base_of, col_of):
                count_one(p, 0, base_of, col_of, True)
                with dve.Fori(1, G) as g:
                    count_one(p, g, base_of, col_of, False)

            NPREP = 7

            def prepare(p, g, s, first2, base_of, col_of):
                n = (p * G + g) * NPREP
                base = base_of(g)
                if not first2:
                    dve.wait_ge(msg_ps, p * G + g - 1)
                nc.vector.scalar_tensor_tensor(out=idx[s][:], in0=grp(srcs, g), scalar=float(R), in1=grp(ets, g),
                                               op0=ALU.mult, op1=ALU.add).then_inc(idx_rdy, 1)
                local_dst(g, s, col_of(g)).then_inc(prep_step, 1)
                nc.vector.tensor_scalar(cf[:, 0, :], CT[:, bass.ds(base, WIN)], 1.0, None,
                                        ALU.max).then_inc(prep_step, 1)
                dve.wait_ge(prep_step, n + 2)
                nc.vector.reciprocal(cf[:, 1, :], cf[:, 0, :]).then_inc(prep_step, 1)
                dve.wait_ge(prep_step, n + 3)
                nc.vector.tensor_copy(cinv[:, s, 0, :], cf[:, 1, :]).then_inc(prep_step, 1)
                dve.wait_ge(prep_step, n + 4)
                nc.vector.tensor_tensor(cf[:, 2, :], cf[:, 1, :], cinv[:, s, 0, :], ALU.subtract
                                        ).then_inc(prep_step, 1)
                dve.wait_ge(prep_step, n + 5)
                nc.vector.tensor_copy(cinv[:, s, 1, :], cf[:, 2, :]).then_inc(prep_step, 1)
                dve.wait_ge(prep_step, n + 6)
                nc.vector.tensor_tensor(cinv[:, s, 2, :], cf[:, 2, :], cinv[:, s, 1, :], ALU.subtract
                                        ).then_inc(prep_step, 1)
                if isinstance(g, int):
                    dve.wait_ge(etb_in[s], p * (G // 2) * 16 + (g // 2 + 1) * 16)
                else:
                    dve.wait_ge(etb_in[s], (p * (G // 2) + (g - s) // 2 + 1) * 16)
                dve.wait_ge(prep_step, n + 7)
                nc.vector.tensor_scalar(rel1h[:, s, :], etb[:, s, :], pidx[0:R, :], None,
                                        ALU.is_equal).then_inc(rel_rdy, 1)

            def weigh(p, g, s):
                for k in range(CH):
                    if k % 4 == 0:
                        dve.wait_ge(look_ps, (p * G + g) * 4 + k // 4 + 1)
                    nc.vector.scalar_tensor_tensor(
                        out=wts[:, s, k, :], in0=iota_n[:], scalar=dloc2[:, s, k:k + 1],
                        in1=bank[k // 4][:, (k % 4) * WIN:(k % 4 + 1) * WIN],
                        op0=ALU.is_equal, op1=ALU.mult).then_inc(wts_rdy, 1)

            def add_messages(p, g, s, base, first):
                if not first:
                    dve.wait_ge(msg_add, p * G + g)
                dve.wait_ge(msg_ps, p * G + g + 1)
                w = H[:, bass.ds(base, WIN)]
                nc.vector.tensor_tensor(w, w, acc_ps[s][:, 0:WIN], ALU.add).then_inc(msg_add, 1)

            def message_pass(p, base_of, col_of):
                prepare(p, 0, 0, True, base_of, col_of)
                prepare(p, 1, 1, True, base_of, col_of)
                base = base_of(0)
                weigh(p, 0, 0)
                add_messages(p, 0, 0, base, True)
                with dve.Fori(0, (G - 2) // 2) as j:
                    for u in (1, 2):
                        g = 2 * j + u
                        prepare(p, g + 1, (u + 1) % 2, False, base_of, col_of)
                        base = base_of(g)
                        weigh(p, g, u % 2)
                        add_messages(p, g, u % 2, base, False)
                base = base_of(G - 1)
                weigh(p, G - 1, 1)
                add_messages(p, G - 1, 1, base, False)

            def fast():
                count_pass(0, fast_base, fast_col)
                dve.wait_ge(cnt_add, G)
                dve.wait_ge(root_out, NT)
                message_pass(0, fast_base, fast_col)

            def general():
                def bases(p):
                    return lambda g: p * WIN, lambda g: passb[:, bass.ds(p, 1)]

                general_passes(dve, lambda p: count_pass(p, *bases(p)), lambda p: dve.wait_ge(cnt_add, (p + 1) * G))
                dve.wait_ge(root_out, NT)
                general_passes(dve, lambda p: message_pass(p, *bases(p)), lambda p: dve.wait_ge(msg_add, (p + 1) * G))

            both_paths(dve, fast, general)
            dve.wait_ge(msg_add, G)

            k0 = 6
            for c in range(N // BNC):
                nc.vector.bn_stats(bst[:, c, :], H[:, c * BNC:(c + 1) * BNC]).then_inc(dve_step, 1)
            k0 += N // BNC
            dve.wait_ge(dve_step, k0)
            nc.vector.bn_aggr(col(MV, 2), bst[:].rearrange("p c s -> p (c s)")).then_inc(dve_step, 1)
            dve.wait_ge(dve_step, k0 + 1)
            nc.vector.tensor_scalar(col(STD), col(MV + 1), EPS, None, ALU.add).then_inc(norm_rdy, 1)
            dve.wait_ge(std_rdy, 1)
            nc.vector.reciprocal(col(SCL), col(STD)).then_inc(dve_step, 1)
            dve.wait_ge(dve_step, k0 + 2)
            nc.vector.tensor_tensor(col(SCL), col(SCL), col(GAM), ALU.mult).then_inc(dve_step, 1)
            dve.wait_ge(dve_step, k0 + 3)
            nc.vector.tensor_tensor(col(SHF), col(MV), col(SCL), ALU.mult).then_inc(dve_step, 1)
            dve.wait_ge(dve_step, k0 + 4)
            nc.vector.tensor_tensor(col(SHF), col(BET), col(SHF), ALU.subtract).then_inc(norm_rdy, 1)

            def begin(b):
                s = b % 2
                dve.wait_ge(xr_in[s], 16 * (b // 2 + 1) + (16 if b == NB - 1 else 0))
                for t in range(BG):
                    i = b * BG + t
                    n = NLAST if i == NT - 1 else P
                    dve.wait_ge(tr_done, i + 1)
                    nc.vector.tensor_tensor(zo[s][0:n, t, :], xin[s][0:n, t, :], bank[i % 4][0:n, 0:P],
                                            ALU.add).then_inc(z_add, 1)
                for t in range(BG):
                    i = b * BG + t
                    n = NLAST if i == NT - 1 else P
                    dve.wait_ge(z_add, i + 1)
                    nc.vector.bn_stats(lst[s][0:n, t, :], zo[s][0:n, t, :]).then_inc(fin_step, 1)
                for t in range(BG):
                    n = NLAST if b * BG + t == NT - 1 else P
                    dve.wait_ge(fin_step, step[0] + t + 1)
                    nc.vector.bn_aggr(lmv[s][0:n, t, :], lst[s][0:n, t, :]).then_inc(fin_step, 1)
                step[0] += 2 * BG
                dve.wait_ge(fin_step, step[0])
                nc.vector.tensor_scalar(lrs[s][:, 0, :], lmv[s][:, :, 1], EPS, None, ALU.add).then_inc(lv_rdy, 1)

            def end(b):
                s = b % 2
                dve.wait_ge(lstd_rdy, b + 1)
                nc.vector.reciprocal(lrs[s][:, 2, :], lrs[s][:, 1, :]).then_inc(fin_step, 1)
                step[0] += 1
                dve.wait_ge(fin_step, step[0])
                if b >= 2:
                    dve.wait_ge(o_out[s], 16 * (b // 2))
                for t in range(BG):
                    n = NLAST if b * BG + t == NT - 1 else P
                    ins = nc.vector.tensor_scalar(oo[s][0:n, t, :], zo[s][0:n, t, :], lmv[s][0:n, t, 0:1],
                                                  lrs[s][0:n, 2, t:t + 1], ALU.subtract, ALU.mult)
                ins.then_inc(o_rdy, 1)

            step = [0]
            nc.vector.memset(lmv[(NB - 1) % 2], 1.0).then_inc(fin_step, 1)
            step[0] += 1
            dve.wait_ge(fin_step, 1)
            begin(0)
            for b in range(1, NB):
                begin(b)
                end(b - 1)
            end(NB - 1)


_INS = ['x', 'src', 'dst', 'edge_type_65', 'L0_gnn_W_rel', 'L0_gnn_W_root', 'L0_gnn_bias', 'L0_gnn_W_res',
        'L0_gnn_b_res', 'L0_gnn_gamma', 'L0_gnn_beta']


def kernel(**inputs):
    import numpy as _np
    import concourse.bacc as _bacc
    from concourse import mybir as _mybir
    from concourse.bass_utils import run_bass_kernel_spmd as _run

    nc = _bacc.Bacc("TRN2", target_bir_lowering=False, num_devices=1)
    arrays, args = {}, []
    for name in _INS:
        a = _np.ascontiguousarray(inputs[name])
        arrays[f"in_{name}_dram"] = a
        args.append(nc.dram_tensor(f"in_{name}_dram", a.shape, _mybir.dt.from_np(a.dtype), kind="ExternalInput").ap())
    args.append(nc.dram_tensor("out_0_dram", inputs["x"].shape, _mybir.dt.float32, kind="ExternalOutput").ap())
    gnn(nc, *args)
    r = _run(nc, [arrays], core_ids=[0])
    return r.results[0]["out_0_dram"]
```

```python
from contextlib import ExitStack

import concourse.bass as bass
from concourse import mybir
import numpy as np

F32 = mybir.dt.float32
BF16 = mybir.dt.bfloat16
I32 = mybir.dt.int32
ALU = mybir.AluOpType
ACT = mybir.ActivationFunctionType
AX = mybir.AxisListType

P = 128
CH = 16
WIN = 80
GE = P * CH
RPM = 4
EPS = 1e-5


def ceil_div(a, b):
    return -(-a // b)


def gnn(nc, x, src, dst, et, w_rel, w_root, bias, w_res, b_res, gamma, beta, out):
    N, F = x.shape
    E = src.shape[0]
    R = w_rel.shape[0]
    assert F == P and w_rel.shape[1] == P and w_rel.shape[2] == P
    NT = ceil_div(N, P)
    NLAST = N - (NT - 1) * P
    G = ceil_div(E, GE)
    ELAST = E - (G - 1) * GE
    PLAST = ELAST // CH
    assert ELAST % CH == 0 and G % 2 == 0 and NT % 2 == 1 and G == 2 * NT
    PASSES = ceil_div(N, WIN)
    NPIECE = R // RPM
    assert R == NPIECE * RPM + 1 and NPIECE % 4 == 0
    HC = N + WIN
    assert HC >= NT * P
    BG = 7
    NB = NT // BG
    assert NB * BG == NT and NB > 3
    BNC = 250
    assert N % BNC == 0

    ytab = nc.dram_tensor("ytab", (NT * P * R, F), F32, kind="Internal").ap()
    etpad = nc.dram_tensor("etpad", (G * GE,), BF16, kind="Internal").ap()
    ytab_tiles = ytab.rearrange("(t p r) f -> t p (r f)", p=P, r=R)
    etpad_rows = etpad.rearrange("(g e) -> g e", e=GE)

    with ExitStack() as ctx:
        def sb(name, shape, dt):
            return ctx.enter_context(nc.sbuf_tensor(name, shape, dt))

        def pb(name, shape, dt):
            return ctx.enter_context(nc.psum_tensor(name, shape, dt))

        def sem(name):
            return ctx.enter_context(nc.semaphore(name))

        wall = sb("wall", [P, R * F], F32)
        stage = sb("stage", [P, 2, R * F], F32)
        H = sb("H", [P, HC], F32)
        CT = sb("CT", [R, HC], F32)
        srcs = sb("srcs", [P, G * CH], I32)
        dsts = sb("dsts", [P, G * CH], I32)
        ets = sb("ets", [P, G * CH], I32)
        et16 = sb("et16", [P, G * CH], BF16)
        drow = sb("drow", [1, G], F32)
        basec = sb("basec", [P, G], F32)
        passb = sb("passb", [P, PASSES], F32)
        dloc2 = sb("dloc2", [P, 2, CH], F32)
        idx = [sb(f"idx{s}", [P, CH], I32) for s in range(2)]
        onehot_n = [sb(f"onehot_n{s}", [P, CH, WIN], BF16) for s in range(2)]
        onehot_r = [sb(f"onehot_r{s}", [P, CH, R], BF16) for s in range(2)]
        dcnt = sb("dcnt", [P, 2, CH], F32)
        rel1h = sb("rel1h", [R, 2, GE], BF16)
        wts = sb("wts", [P, 2, CH, WIN], F32)
        cf = sb("cf", [R, 4, WIN], F32)
        cinv = sb("cinv", [R, 2, 3, WIN], BF16)
        xt_in = sb("xt_in", [P, 2, F], F32)
        xT = [sb(f"xT{s}", [P, P], F32) for s in range(2)]
        wroot = sb("wroot", [P, F], F32)
        wres = sb("wres", [P, F], F32)
        ident = sb("ident", [P, P], F32)
        ones = sb("ones", [P, P], F32)
        iota_n = sb("iota_n", [P, WIN], F32)
        iota_r = sb("iota_r", [P, R], F32)
        pidx = sb("pidx", [P, 1], F32)
        cols = sb("cols", [P, 16], F32)
        flag = sb("flag", [1, 1], I32)
        bst = sb("bst", [P, N // BNC, 6], F32)
        etb = wall[0:R, 0:GE].bitcast(BF16).rearrange("r (s e) -> r s e", s=2)
        ys = [stage[:, s, 0:CH * F].rearrange("p (k f) -> p k f", f=F) for s in range(2)]
        xin = [stage[:, s, 2 * BG * F:3 * BG * F].rearrange("p (t f) -> p t f", f=F) for s in range(2)]
        oo = [stage[:, s, 4 * BG * F:5 * BG * F].rearrange("p (t f) -> p t f", f=F) for s in range(2)]
        NS = 3
        lst = sb("lst", [P, NS, BG, 6], F32)
        lmv = sb("lmv", [P, NS, BG, 2], F32)
        lrs = sb("lrs", [P, NS, 4, BG], F32)
        (B_BIAS, B_RES, GAM, BET, BSUM, BAD, MV, STD, SCL, SHF) = (0, 1, 2, 3, 4, 5, 6, 8, 9, 10)
        LO, HI, TWO_ON, ONE_ON = 11, 12, 13, 14

        bank = [pb(f"bank{i}", [P, 512], F32) for i in range(4)]
        root_ps = pb("root_ps", [P, 512], F32)
        tr_ps = pb("tr_ps", [P, 512], F32)
        acc_ps = [pb(f"acc_ps{i}", [P, 512], F32) for i in range(2)]
        cnt_acc = [tr_ps[0:R, 0:WIN], root_ps[0:R, 0:WIN]]
        last_banks = [bank[0], bank[1], bank[2], bank[3], root_ps, tr_ps]

        loaded = {n: sem("loaded_" + n) for n in ("src", "dst", "et", "wroot", "small")}
        wrel_in = [sem(f"wrel_in{q}") for q in range(4)]
        padded = sem("padded")
        pads_in = sem("pads_in")
        consts = sem("consts")
        et16_done = sem("et16_done")
        etpad_in_dram = sem("etpad_in_dram")
        base_row = sem("base_row")
        base_ps = sem("base_ps")
        bad_rdy = sem("bad_rdy")
        bad_ps = sem("bad_ps")
        flag_rdy = sem("flag_rdy")
        dve_step = sem("dve_step")
        x_in = [sem(f"x_in{s}") for s in range(2)]
        xT_ps = sem("xT_ps")
        xT_rdy = sem("xT_rdy")
        piece_ps = sem("piece_ps")
        piece_out = sem("piece_out")
        root_done = sem("root_done")
        root_out = sem("root_out")
        tab_out = [sem(f"tab_out{s}") for s in range(2)]
        oh_rdy = sem("oh_rdy")
        cnt_ps = sem("cnt_ps")
        cnt_add = sem("cnt_add")
        cnt_step = sem("cnt_step")
        etb_in = [sem(f"etb_in{s}") for s in range(2)]
        idx_rdy = sem("idx_rdy")
        prep_step = sem("prep_step")
        rel_rdy = sem("rel_rdy")
        look_ps = sem("look_ps")
        wts_rdy = sem("wts_rdy")
        pool_turn = sem("pool_turn")
        sp_turn = sem("sp_turn")
        gathered = [sem(f"gathered{s}") for s in range(2)]
        msg_ps = sem("msg_ps")
        msg_add = sem("msg_add")
        norm_rdy = sem("norm_rdy")
        std_rdy = sem("std_rdy")
        relu_rdy = sem("relu_rdy")
        sum_ps = sem("sum_ps")
        row_step = sem("row_step")
        lv_rdy = sem("lv_rdy")
        lstd_rdy = sem("lstd_rdy")
        lnorm_rdy = sem("lnorm_rdy")
        o_rdy = sem("o_rdy")
        xr_in = [sem(f"xr_in{s}") for s in range(2)]
        o_out = [sem(f"o_out{s}") for s in range(2)]

        block = ctx.enter_context(nc.Block())

        def rows_ps(b, t):
            return last_banks[2 * (b % NS) + t // 4][:, t % 4 * P:(t % 4 + 1) * P]

        def col(c, n=1):
            return cols[:, c:c + n]

        def colvec(v):
            return v.rearrange("(p a) -> p a", a=1)

        def grp(t, g):
            return t[:, bass.ds(g * CH, CH)]

        def both_paths(eng, fast, general):
            eng.wait_ge(flag_rdy, 1)
            bad = eng.value_load(flag[0:1, 0:1], min_val=0, max_val=P)
            with eng.If(bad == 0):
                fast()
            with eng.Else():
                general()

        def general_passes(eng, one_pass, before_pass):
            with eng.Fori(0, PASSES) as p:
                one_pass(p)
                before_pass(p)

        @block.sync
        def _(sp):
            def load_x(i, s):
                sp.dma_start(xt_in[:, s, :], x[bass.ds(i * P, P), :]).then_inc(x_in[s], 16)

            load_x(0, 0)
            qc = NPIECE // 4 * RPM
            for q in range(4):
                lo, hi = q * qc, (q + 1) * qc if q < 3 else R
                sp.dma_start(wall[:, lo * F:hi * F].rearrange("p (r f) -> p r f", f=F),
                             w_rel[lo:hi, :, :].rearrange("r p f -> p r f")).then_inc(wrel_in[q], 16)
            sp.dma_start(wroot[:], w_root).then_inc(loaded["wroot"], 16)
            sp.dma_start(wres[:], w_res).then_inc(loaded["wroot"], 16)
            for c, v in ((B_BIAS, bias), (B_RES, b_res), (GAM, gamma), (BET, beta)):
                sp.dma_start(col(c), colvec(v)).then_inc(loaded["small"], 16)
            load_x(1, 1)
            for n, t, v in (("et", ets, et), ("dst", dsts, dst), ("src", srcs, src)):
                full = v[0:(G - 1) * GE].rearrange("(g p k) -> p g k", p=P, k=CH)
                sp.dma_start(t[:, 0:(G - 1) * CH].rearrange("p (g k) -> p g k", k=CH), full).then_inc(loaded[n], 16)
                sp.wait_ge(padded, 2)
                sp.dma_start(t[0:PLAST, (G - 1) * CH:G * CH],
                             v[(G - 1) * GE:E].rearrange("(p k) -> p k", k=CH)).then_inc(loaded[n], 16)
            sp.wait_ge(et16_done, 1)
            sp.dma_start(etpad.rearrange("(g p k) -> p g k", p=P, k=CH),
                         et16[:].rearrange("p (g k) -> p g k", k=CH)).then_inc(etpad_in_dram, 16)

            half = NPIECE // 2 * RPM * F

            def store_tile(i, s):
                tile = ytab_tiles[bass.ds(i, 1), :, :].rearrange("t p c -> (t p) c")
                sp.wait_ge(piece_out, i * NPIECE + NPIECE // 2)
                sp.sem_inc(sp_turn)
                sp.dma_start(tile[:, 0:half], stage[:, s, 0:half]).then_inc(tab_out[s], 16)
                sp.wait_ge(piece_out, (i + 1) * NPIECE)
                sp.wait_ge(root_out, i + 1)
                sp.sem_inc(sp_turn)
                sp.dma_start(tile[:, half:], stage[:, s, half:]).then_inc(tab_out[s], 16)

            with sp.Fori(0, (NT - 3) // 2) as j:
                for s in range(2):
                    i = 2 * j + s
                    sp.wait_ge(xT_ps, i + 1)
                    sp.sem_inc(sp_turn)
                    load_x(i + 2, s)
                    store_tile(i, s)
            for i in range(NT - 3, NT):
                if i + 2 < NT:
                    sp.wait_ge(xT_ps, i + 1)
                if i + 2 < NT - 1:
                    load_x(i + 2, i % 2)
                elif i + 2 == NT - 1:
                    sp.wait_ge(padded, 3)
                    sp.dma_start(xt_in[0:NLAST, i % 2, :], x[(NT - 1) * P:N, :]).then_inc(x_in[i % 2], 16)
                store_tile(i, i % 2)

            sp.wait_ge(etpad_in_dram, 16)

            def load_etb(p, g, s, first):
                if not first:
                    sp.wait_ge(rel_rdy, p * G + g - 1)
                    sp.sem_inc(sp_turn)
                sp.dma_start(etb[:, s, :], etpad_rows[bass.ds(g, 1), :].to_broadcast([R, GE])).then_inc(etb_in[s], 16)

            def etb_pass(p):
                for s in range(2):
                    load_etb(p, s, s, True)
                with sp.Fori(1, G // 2) as j:
                    for s in range(2):
                        load_etb(p, 2 * j + s, s, False)

            def general_after(p):
                sp.wait_ge(msg_add, (p + 1) * G)
                sp.sem_inc(sp_turn)

            both_paths(sp, lambda: etb_pass(0), lambda: general_passes(sp, etb_pass, general_after))

            def rows(t, b, n):
                return t[bass.ds(b * BG * P, n * P), :].rearrange("(t p) f -> p t f", p=P)

            def load_res(b, s):
                if isinstance(b, int) and b == NB - 1:
                    sp.dma_start(xin[s][:, 0:BG - 1, :], rows(x, b, BG - 1)).then_inc(xr_in[s], 16)
                    sp.dma_start(xin[s][0:NLAST, BG - 1, :], x[(NT - 1) * P:N, :]).then_inc(xr_in[s], 16)
                else:
                    sp.dma_start(xin[s], rows(x, b, BG)).then_inc(xr_in[s], 16)

            sp.wait_ge(norm_rdy, 1)
            load_res(0, 0)
            load_res(1, 1)
            for b in range(NB):
                s = b % 2
                if b + 2 < NB:
                    sp.wait_ge(sum_ps, (b + 1) * BG)
                    load_res(b + 2, s)
                sp.wait_ge(o_rdy, b + 1)
                if b < NB - 1:
                    sp.dma_start(rows(out, b, BG), oo[s]).then_inc(o_out[s], 16)
                else:
                    sp.dma_start(rows(out, b, BG - 1), oo[s][:, 0:BG - 1, :]).then_inc(o_out[s], 16)
                    sp.dma_start(out[(NT - 1) * P:N, :], oo[s][0:NLAST, BG - 1, :]).then_inc(o_out[s], 16)
            sp.wait_ge(o_out[(NB - 1) % 2], 16 * ((NB + 1) // 2 + 1))
            sp.wait_ge(o_out[NB % 2], 16 * (NB // 2))

        @block.gpsimd
        def _(pool):
            nc.gpsimd.memset(ets[:, (G - 1) * CH:G * CH], -1).then_inc(padded, 1)
            nc.gpsimd.memset(srcs[:, (G - 1) * CH:G * CH], 1).then_inc(padded, 1)
            pool.dma_start(dsts[PLAST:P, (G - 1) * CH:G * CH],
                           dst[E - CH:E].rearrange("(a k) -> a k", a=1).to_broadcast([P - PLAST, CH])).then_inc(pads_in, 16)
            nc.gpsimd.memset(ones[:], 1.0).then_inc(consts, 1)
            pool.wait_ge(consts, 1)
            nc.gpsimd.affine_select(out=ident[:], in_=ones[:], compare_op=ALU.is_equal, fill=0.0, base=0,
                                    pattern=[[-1, P]], channel_multiplier=1).then_inc(consts, 1)
            nc.gpsimd.iota(iota_n[:], [[1, WIN]], base=0, channel_multiplier=0,
                           allow_small_or_imprecise_dtypes=True).then_inc(consts, 1)
            nc.gpsimd.iota(iota_r[:], [[1, R]], base=0, channel_multiplier=0,
                           allow_small_or_imprecise_dtypes=True).then_inc(consts, 1)
            nc.gpsimd.iota(pidx[:], [[1, 1]], base=0, channel_multiplier=1,
                           allow_small_or_imprecise_dtypes=True).then_inc(consts, 1)
            nc.gpsimd.iota(passb[:], [[WIN, PASSES]], base=0, channel_multiplier=0,
                           allow_small_or_imprecise_dtypes=True).then_inc(consts, 1)
            nc.gpsimd.memset(CT[:], 0.0).then_inc(consts, 1)
            nc.gpsimd.memset(H[:, NT * P:HC], 0.0).then_inc(consts, 1)
            pool.wait_ge(xT_ps, NT - 2)
            nc.gpsimd.memset(xt_in[:, (NT - 1) % 2, :], 0.0).then_inc(padded, 1)

            for s in range(2):
                pool.wait_ge(tab_out[s], 32 * ((NT + 1 - s) // 2))

            def gather(p, g, s, first):
                pool.wait_ge(idx_rdy, p * G + g + 1)
                if not first:
                    pool.wait_ge(msg_ps, p * G + g - 1)
                pool.sem_inc(pool_turn)
                for k in range(CH):
                    pool.indirect_dma_start(
                        out=ys[s][:, k, :], out_offset=None, in_=ytab,
                        in_offset=bass.IndirectOffsetOnAxis(ap=idx[s][:, k:k + 1], axis=0)).then_inc(gathered[s], 16)

            def gather_pass(p):
                for s in range(2):
                    gather(p, s, s, True)
                with pool.Fori(1, G // 2) as j:
                    for s in range(2):
                        gather(p, 2 * j + s, s, False)

            def general_after(p):
                pool.wait_ge(msg_add, (p + 1) * G)
                pool.sem_inc(pool_turn)

            both_paths(pool, lambda: gather_pass(0), lambda: general_passes(pool, gather_pass, general_after))

        @block.tensor
        def _(pe):
            def spread_bases():
                pe.wait_ge(base_row, 1)
                nc.tensor.matmul(acc_ps[0][:, 0:G], ones[0:1, :], drow[:], start=True, stop=True).then_inc(base_ps, 1)

            def sum_bad():
                pe.wait_ge(bad_rdy, 1)
                nc.tensor.matmul(acc_ps[0][0:1, G:G + 1], col(BAD), ones[:, 0:1], start=True, stop=True).then_inc(bad_ps, 1)

            def transpose_x(i, s, first, last):
                pe.wait_ge(x_in[s], 8 * (i - s) + 16)
                if not first:
                    pe.wait_ge(xT_rdy, i)
                nc.tensor.transpose(tr_ps[:, 0:P], xt_in[:, s, :], ident[:]).then_inc(xT_ps, 1)

            def table_tile(i, s, first, last):
                if not last:
                    transpose_x(i + 1, 1 - s, False, False)
                pe.wait_ge(xT_rdy, i + 1)
                for q in range(NPIECE):
                    if not (first and q < 4):
                        pe.wait_ge(piece_out, i * NPIECE + q - 3)
                    if first and q % 4 == 0:
                        pe.wait_ge(wrel_in[q // 4], 16)
                    nc.tensor.matmul(bank[q % 4][:], xT[s][:], wall[:, q * 512:(q + 1) * 512],
                                     start=True, stop=True).then_inc(piece_ps, 1)
                    if q == 13:
                        if first:
                            pe.wait_ge(loaded["wroot"], 32)
                        if not first:
                            pe.wait_ge(root_out, i)
                        nc.tensor.matmul(root_ps[:, P:2 * P], xT[s][:], wall[:, NPIECE * 512:],
                                         start=True, stop=True)
                        nc.tensor.matmul(root_ps[:, 0:P], wroot[:], xT[s][:], start=True, stop=False)
                        nc.tensor.matmul(root_ps[:, 0:P], wres[:], xT[s][:], start=False,
                                         stop=True).then_inc(root_done, 1)

            def count_group(p, g, s, first2):
                pe.wait_ge(oh_rdy, p * G + g + 1)
                if not first2:
                    pe.wait_ge(cnt_add, p * G + g - 1)
                for k in range(CH):
                    ins = nc.tensor.matmul(cnt_acc[s], onehot_r[s][:, k, :], onehot_n[s][:, k, :],
                                           start=(k == 0), stop=(k == CH - 1))
                ins.then_inc(cnt_ps, 1)

            pe.wait_ge(consts, 2)
            transpose_x(0, 0, True, False)
            table_tile(0, 0, True, False)
            with pe.Fori(0, (NT - 3) // 2) as j:
                for u in (1, 2):
                    table_tile(2 * j + u, u % 2, False, False)
            spread_bases()
            table_tile(NT - 2, 1, False, False)
            sum_bad()
            table_tile(NT - 1, 0, False, True)
            pe.wait_ge(piece_out, NT * NPIECE)
            pe.wait_ge(root_out, NT)

            def count_pass(p):
                for g in range(2):
                    count_group(p, g, g, True)
                with pe.Fori(1, G // 2) as j:
                    for s in range(2):
                        count_group(p, 2 * j + s, s, False)

            def count_after(p):
                pe.wait_ge(cnt_add, (p + 1) * G)

            def lookup(p, g, s, first):
                pe.wait_ge(rel_rdy, p * G + g + 1)
                rel = rel1h[:, s, :].rearrange("r (p k) -> r k p", k=CH)
                for b in range(4):
                    if not first:
                        pe.wait_ge(wts_rdy, (p * G + g - 1) * CH + 4 * b + 4)
                    for k in range(4 * b, 4 * b + 4):
                        for part in range(3):
                            ins = nc.tensor.matmul(bank[b][:, (k - 4 * b) * WIN:(k - 4 * b + 1) * WIN],
                                                   rel[:, k, :], cinv[:, s, part, :],
                                                   start=(part == 0), stop=(part == 2))
                    ins.then_inc(look_ps, 1)

            def messages(p, g, s, first2):
                pe.wait_ge(gathered[s], (p * (G // 2) + (g - s) // 2 + 1) * 16 * CH if not isinstance(g, int)
                           else p * (G // 2) * 16 * CH + (g // 2 + 1) * 16 * CH)
                if not first2:
                    pe.wait_ge(msg_add, p * G + g - 1)
                for k in range(CH):
                    pe.wait_ge(wts_rdy, (p * G + g) * CH + k + 1)
                    ins = nc.tensor.matmul(acc_ps[s][:, 0:WIN], ys[s][:, k, :], wts[:, s, k, :],
                                           start=(k == 0), stop=(k == CH - 1))
                ins.then_inc(msg_ps, 1)

            def message_group(p, g, s, count):
                lookup(p, g, s, isinstance(g, int) and g == 0)
                if count:
                    count_group(p, g + 3, 1 - s, False)
                messages(p, g, s, isinstance(g, int) and g < 2)

            def message_pass(p, count):
                for g in range(3):
                    message_group(p, g, g % 2, count)
                with pe.Fori(0, (G - 6) // 2) as j:
                    for u in (3, 4):
                        message_group(p, 2 * j + u, u % 2, count)
                for g in range(G - 3, G):
                    message_group(p, g, g % 2, False)

            def general_after(p):
                pe.wait_ge(msg_add, (p + 1) * G)

            def fast():
                for g in range(3):
                    count_group(0, g, g % 2, g < 2)
                message_pass(0, True)

            def general():
                general_passes(pe, count_pass, count_after)
                general_passes(pe, lambda p: message_pass(p, False), general_after)

            both_paths(pe, fast, general)

            for b in range(NB):
                pe.wait_ge(relu_rdy, b + 1)
                pe.wait_ge(xr_in[b % 2], 16 * (b // 2 + 1) + (16 if b == NB - 1 else 0))
                if b >= NS:
                    pe.wait_ge(o_rdy, b - NS + 1)
                for t in range(BG):
                    i = b * BG + t
                    n = NLAST if i == NT - 1 else P
                    nc.tensor.matmul(rows_ps(b, t)[0:n, :], H[:, i * P:i * P + n], ident[:], start=True, stop=False)
                    nc.tensor.matmul(rows_ps(b, t)[0:n, :], ident[0:n, 0:n], xin[b % 2][0:n, t, :],
                                     start=False, stop=True).then_inc(sum_ps, 1)

        @block.scalar
        def _(act):
            def tile(i, s, first2):
                act.wait_ge(xT_ps, i + 1)
                nc.scalar.activation(xT[s][:], tr_ps[:, 0:P], ACT.Copy).then_inc(xT_rdy, 1)
                if not first2:
                    act.wait_ge(tab_out[s], 16 * (i - s))
                for q in range(NPIECE):
                    act.wait_ge(piece_ps, i * NPIECE + q + 1)
                    nc.scalar.activation(stage[:, s, q * 512:(q + 1) * 512], bank[q % 4][:],
                                         ACT.Copy).then_inc(piece_out, 1)
                act.wait_ge(root_done, i + 1)
                nc.scalar.activation(H[:, bass.ds(i * P, P)], root_ps[:, 0:P], ACT.Identity, bias=col(BSUM))
                nc.scalar.activation(stage[:, s, NPIECE * 512:], root_ps[:, P:2 * P],
                                     ACT.Copy).then_inc(root_out, 1)

            act.wait_ge(dve_step, 1)
            tile(0, 0, True)
            tile(1, 1, True)
            with act.Fori(1, NT // 2) as j:
                for s in range(2):
                    tile(2 * j + s, s, False)
            tile(NT - 1, 0, False)

            act.wait_ge(norm_rdy, 1)
            nc.scalar.activation(col(STD), col(STD), ACT.Sqrt).then_inc(std_rdy, 1)
            act.wait_ge(norm_rdy, 2)

            def relu(b):
                h = H[:, b * BG * P:(b + 1) * BG * P]
                nc.scalar.activation(h, h, ACT.Relu, bias=col(SHF), scale=col(SCL)).then_inc(relu_rdy, 1)

            def root_of(b):
                act.wait_ge(lv_rdy, b + 1)
                nc.scalar.activation(lrs[:, b % NS, 1, :], lrs[:, b % NS, 0, :], ACT.Sqrt).then_inc(lstd_rdy, 1)

            def scale_rows(b):
                act.wait_ge(lnorm_rdy, b + 1)
                if b >= 2:
                    act.wait_ge(o_out[b % 2], 16 * (b // 2))
                for t in range(BG):
                    n = NLAST if b * BG + t == NT - 1 else P
                    ins = nc.scalar.activation(oo[b % 2][0:n, t, :], rows_ps(b, t)[0:n, :], ACT.Identity,
                                               bias=lrs[0:n, b % NS, 3, t:t + 1], scale=lrs[0:n, b % NS, 2, t:t + 1])
                ins.then_inc(o_rdy, 1)

            relu(0)
            relu(1)
            for b in range(NB):
                if b + 2 < NB:
                    relu(b + 2)
                root_of(b)
                if b >= 1:
                    scale_rows(b - 1)
            scale_rows(NB - 1)

        @block.vector
        def _(dve):
            dve.wait_ge(loaded["small"], 64)
            nc.vector.tensor_tensor(col(BSUM), col(B_BIAS), col(B_RES), ALU.add).then_inc(dve_step, 1)
            dve.wait_ge(loaded["et"], 32)
            nc.vector.tensor_copy(et16[:], ets[:]).then_inc(et16_done, 1)
            dve.wait_ge(loaded["dst"], 32)
            dve.wait_ge(loaded["src"], 32)
            dve.wait_ge(pads_in, 16)
            nc.vector.tensor_copy(drow[:], dsts[0:1, :].rearrange("p (g k) -> p g k", k=CH)[:, :, 0]
                                  ).then_inc(base_row, 1)
            dve.wait_ge(base_ps, 1)
            nc.vector.tensor_copy(basec[:], acc_ps[0][:, 0:G]).then_inc(dve_step, 1)
            dve.wait_ge(dve_step, 2)
            scratch = wts[:].rearrange("p s k w -> p (s k w)")
            d3 = dsts[:].rearrange("p (g k) -> p g k", k=CH)
            local, ahead, rise = scratch[:, 0:G * CH], scratch[:, 0:(G - 2) * CH], scratch[:, 0:G - 1]

            def bases_k(g0, n):
                return basec[:, g0:g0 + n].rearrange("p (g a) -> p g a", a=1).to_broadcast([P, n, CH])

            nc.vector.tensor_tensor(local.rearrange("p (g k) -> p g k", k=CH), d3, bases_k(0, G),
                                    ALU.subtract).then_inc(dve_step, 1)
            dve.wait_ge(dve_step, 3)
            nc.vector.tensor_reduce(col(HI), local, AX.X, ALU.max).then_inc(dve_step, 1)
            nc.vector.tensor_reduce(col(LO), local, AX.X, ALU.min).then_inc(dve_step, 1)
            dve.wait_ge(dve_step, 5)
            nc.vector.tensor_tensor(ahead.rearrange("p (g k) -> p g k", k=CH), d3[:, 0:G - 2, :],
                                    bases_k(2, G - 2), ALU.subtract).then_inc(dve_step, 1)
            dve.wait_ge(dve_step, 6)
            nc.vector.tensor_reduce(col(TWO_ON), ahead, AX.X, ALU.max).then_inc(dve_step, 1)
            dve.wait_ge(dve_step, 7)
            nc.vector.tensor_tensor(rise, basec[:, 1:G], basec[:, 0:G - 1], ALU.subtract).then_inc(dve_step, 1)
            dve.wait_ge(dve_step, 8)
            nc.vector.tensor_reduce(col(ONE_ON), rise, AX.X, ALU.min).then_inc(dve_step, 1)
            nc.vector.tensor_scalar(col(HI), col(HI), float(WIN - 1), None, ALU.is_gt).then_inc(dve_step, 1)
            nc.vector.tensor_scalar(col(TWO_ON), col(TWO_ON), 0.0, None, ALU.is_ge).then_inc(dve_step, 1)
            dve.wait_ge(dve_step, 11)
            nc.vector.scalar_tensor_tensor(out=col(HI), in0=col(LO), scalar=0.0, in1=col(HI), op0=ALU.is_lt,
                                           op1=ALU.max).then_inc(dve_step, 1)
            nc.vector.scalar_tensor_tensor(out=col(TWO_ON), in0=col(ONE_ON), scalar=0.0, in1=col(TWO_ON),
                                           op0=ALU.is_lt, op1=ALU.max).then_inc(dve_step, 1)
            dve.wait_ge(dve_step, 13)
            nc.vector.tensor_tensor(col(BAD), col(HI), col(TWO_ON), ALU.max).then_inc(bad_rdy, 1)
            dve.wait_ge(bad_ps, 1)
            nc.vector.tensor_copy(flag[:], acc_ps[0][0:1, G:G + 1]).then_inc(flag_rdy, 1)
            dve.wait_ge(consts, 8)

            def bcast_k(t2, n):
                return t2.rearrange("p (k a) -> p k a", a=1).to_broadcast([t2.shape[0], CH, n])

            def bcast_n(t2, n):
                return t2.rearrange("p (a n) -> p a n", a=1).to_broadcast([t2.shape[0], CH, n])

            def local_dst(out, g, base_col):
                return nc.vector.tensor_tensor(out, grp(dsts, g), base_col.to_broadcast([P, CH]),
                                               ALU.subtract)

            def count_build(p, g, s, base_col, first2):
                n = (p * G + g) * 2
                if not first2:
                    dve.wait_ge(cnt_ps, p * G + g - 1)
                local_dst(dcnt[:, s, :], g, base_col).then_inc(cnt_step, 1)
                nc.vector.tensor_tensor(onehot_r[s][:], bcast_n(iota_r[:], R), bcast_k(grp(ets, g), R),
                                        ALU.is_equal).then_inc(cnt_step, 1)
                dve.wait_ge(cnt_step, n + 2)
                nc.vector.tensor_tensor(onehot_n[s][:], bcast_n(iota_n[:], WIN), bcast_k(dcnt[:, s, :], WIN),
                                        ALU.is_equal).then_inc(oh_rdy, 1)

            def count_sum(p, g, s, base, first):
                if not first:
                    dve.wait_ge(cnt_add, p * G + g)
                dve.wait_ge(cnt_ps, p * G + g + 1)
                w = CT[:, bass.ds(base, WIN)]
                nc.vector.tensor_tensor(w, w, cnt_acc[s], ALU.add).then_inc(cnt_add, 1)

            def fast_base(g):
                return dve.value_load(dsts[0:1, bass.ds(g * CH, 1)], min_val=0, max_val=N - 1)

            def fast_col(g):
                return basec[:, bass.ds(g, 1)]

            def count_pass(p, base_of, col_of):
                count_build(p, 0, 0, col_of(0), True)
                base = base_of(0)
                count_build(p, 1, 1, col_of(1), True)
                count_sum(p, 0, 0, base, True)
                with dve.Fori(0, (G - 2) // 2) as j:
                    for u in (1, 2):
                        g = 2 * j + u
                        base = base_of(g)
                        count_build(p, g + 1, (u + 1) % 2, col_of(g + 1), False)
                        count_sum(p, g, u % 2, base, False)
                base = base_of(G - 1)
                count_sum(p, G - 1, 1, base, False)

            NPREP = 7

            def prepare(p, g, s, first2, base_of, col_of, counted):
                n = (p * G + g) * NPREP
                base = base_of(g)
                if not first2:
                    dve.wait_ge(msg_ps, p * G + g - 1)
                nc.vector.scalar_tensor_tensor(out=idx[s][:], in0=grp(srcs, g), scalar=float(R), in1=grp(ets, g),
                                               op0=ALU.mult, op1=ALU.add).then_inc(idx_rdy, 1)
                local_dst(dloc2[:, s, :], g, col_of(g)).then_inc(prep_step, 1)
                dve.wait_ge(cnt_add, counted)
                nc.vector.tensor_scalar(cf[:, 0, :], CT[:, bass.ds(base, WIN)], 1.0, None,
                                        ALU.max).then_inc(prep_step, 1)
                dve.wait_ge(prep_step, n + 2)
                nc.vector.reciprocal(cf[:, 1, :], cf[:, 0, :]).then_inc(prep_step, 1)
                dve.wait_ge(prep_step, n + 3)
                nc.vector.tensor_copy(cinv[:, s, 0, :], cf[:, 1, :]).then_inc(prep_step, 1)
                dve.wait_ge(prep_step, n + 4)
                nc.vector.tensor_tensor(cf[:, 2, :], cf[:, 1, :], cinv[:, s, 0, :], ALU.subtract
                                        ).then_inc(prep_step, 1)
                dve.wait_ge(prep_step, n + 5)
                nc.vector.tensor_copy(cinv[:, s, 1, :], cf[:, 2, :]).then_inc(prep_step, 1)
                dve.wait_ge(prep_step, n + 6)
                nc.vector.tensor_tensor(cinv[:, s, 2, :], cf[:, 2, :], cinv[:, s, 1, :], ALU.subtract
                                        ).then_inc(prep_step, 1)
                if isinstance(g, int):
                    dve.wait_ge(etb_in[s], p * (G // 2) * 16 + (g // 2 + 1) * 16)
                else:
                    dve.wait_ge(etb_in[s], (p * (G // 2) + (g - s) // 2 + 1) * 16)
                dve.wait_ge(prep_step, n + 7)
                nc.vector.tensor_scalar(rel1h[:, s, :], etb[:, s, :], pidx[0:R, :], None,
                                        ALU.is_equal).then_inc(rel_rdy, 1)

            def weigh(p, g, s):
                for k in range(CH):
                    if k % 4 == 0:
                        dve.wait_ge(look_ps, (p * G + g) * 4 + k // 4 + 1)
                    nc.vector.scalar_tensor_tensor(
                        out=wts[:, s, k, :], in0=iota_n[:], scalar=dloc2[:, s, k:k + 1],
                        in1=bank[k // 4][:, (k % 4) * WIN:(k % 4 + 1) * WIN],
                        op0=ALU.is_equal, op1=ALU.mult).then_inc(wts_rdy, 1)

            def add_messages(p, g, s, base, first):
                if not first:
                    dve.wait_ge(msg_add, p * G + g)
                dve.wait_ge(msg_ps, p * G + g + 1)
                w = H[:, bass.ds(base, WIN)]
                nc.vector.tensor_tensor(w, w, acc_ps[s][:, 0:WIN], ALU.add).then_inc(msg_add, 1)

            def message_group(p, g, s, base_of, col_of, count, prep, count_all):
                first = isinstance(g, int) and g == 0
                if count >= 1:
                    count_sum(p, g + 2, s, base_of(g + 2), False)
                if count >= 2:
                    count_build(p, g + 3, 1 - s, col_of(g + 3), False)
                if prep:
                    ahead = g + 3 if count_all is None else count_all
                    prepare(p, g + 1, 1 - s, first, base_of, col_of, min(ahead, G) if isinstance(ahead, int) and
                            count_all is None else ahead)
                base = base_of(g)
                weigh(p, g, s)
                add_messages(p, g, s, base, first)

            def message_pass(p, base_of, col_of, count, count_all):
                prepare(p, 0, 0, True, base_of, col_of, 2 if count_all is None else count_all)
                for g in range(3):
                    message_group(p, g, g % 2, base_of, col_of, 2 * count, True, count_all)
                with dve.Fori(0, (G - 6) // 2) as j:
                    for u in (3, 4):
                        message_group(p, 2 * j + u, u % 2, base_of, col_of, 2 * count, True, count_all)
                for g in range(G - 3, G):
                    message_group(p, g, g % 2, base_of, col_of, count * (g + 2 < G), g + 1 < G, count_all)

            def fast():
                for g in range(3):
                    count_build(0, g, g % 2, fast_col(g), g < 2)
                    if g >= 1:
                        count_sum(0, g - 1, (g - 1) % 2, fast_base(g - 1), g == 1)
                dve.wait_ge(root_out, NT)
                message_pass(0, fast_base, fast_col, 1, None)

            def general():
                def bases(p):
                    return lambda g: p * WIN, lambda g: passb[:, bass.ds(p, 1)]

                general_passes(dve, lambda p: count_pass(p, *bases(p)), lambda p: dve.wait_ge(cnt_add, (p + 1) * G))
                dve.wait_ge(root_out, NT)
                general_passes(dve, lambda p: message_pass(p, *bases(p), 0, PASSES * G), lambda p: dve.wait_ge(msg_add, (p + 1) * G))

            both_paths(dve, fast, general)
            dve.wait_ge(msg_add, G)

            k0 = 13
            for c in range(N // BNC):
                nc.vector.bn_stats(bst[:, c, :], H[:, c * BNC:(c + 1) * BNC]).then_inc(dve_step, 1)
            k0 += N // BNC
            dve.wait_ge(dve_step, k0)
            nc.vector.bn_aggr(col(MV, 2), bst[:].rearrange("p c s -> p (c s)")).then_inc(dve_step, 1)
            dve.wait_ge(dve_step, k0 + 1)
            nc.vector.tensor_scalar(col(STD), col(MV + 1), EPS, None, ALU.add).then_inc(norm_rdy, 1)
            dve.wait_ge(std_rdy, 1)
            nc.vector.reciprocal(col(SCL), col(STD)).then_inc(dve_step, 1)
            dve.wait_ge(dve_step, k0 + 2)
            nc.vector.tensor_tensor(col(SCL), col(SCL), col(GAM), ALU.mult).then_inc(dve_step, 1)
            dve.wait_ge(dve_step, k0 + 3)
            nc.vector.tensor_tensor(col(SHF), col(MV), col(SCL), ALU.mult).then_inc(dve_step, 1)
            dve.wait_ge(dve_step, k0 + 4)
            nc.vector.tensor_tensor(col(SHF), col(BET), col(SHF), ALU.subtract).then_inc(norm_rdy, 1)

            def row_stats(b):
                s = b % NS
                if b >= NS:
                    dve.wait_ge(o_rdy, b - NS + 1)
                for t in range(BG):
                    n = NLAST if b * BG + t == NT - 1 else P
                    if t % 4 == 0:
                        dve.wait_ge(sum_ps, b * BG + min(t + 4, BG))
                    nc.vector.bn_stats(lst[0:n, s, t, :], rows_ps(b, t)[0:n, :]).then_inc(row_step, 1)
                for t in range(BG):
                    n = NLAST if b * BG + t == NT - 1 else P
                    dve.wait_ge(row_step, step[0] + t + 1)
                    nc.vector.bn_aggr(lmv[0:n, s, t, :], lst[0:n, s, t, :]).then_inc(row_step, 1)
                step[0] += 2 * BG
                dve.wait_ge(row_step, step[0])
                nc.vector.tensor_scalar(lrs[:, s, 0, :], lmv[:, s, :, 1], EPS, None, ALU.add).then_inc(lv_rdy, 1)

            def row_scales(b):
                s = b % NS
                dve.wait_ge(lstd_rdy, b + 1)
                nc.vector.reciprocal(lrs[:, s, 2, :], lrs[:, s, 1, :]).then_inc(row_step, 1)
                step[0] += 1
                dve.wait_ge(row_step, step[0])
                nc.vector.scalar_tensor_tensor(out=lrs[:, s, 3, :], in0=lmv[:, s, :, 0], scalar=-1.0,
                                               in1=lrs[:, s, 2, :], op0=ALU.mult, op1=ALU.mult).then_inc(lnorm_rdy, 1)

            step = [0]
            row_stats(0)
            for b in range(1, NB):
                row_stats(b)
                row_scales(b - 1)
            row_scales(NB - 1)


_INS = ['x', 'src', 'dst', 'edge_type_65', 'L0_gnn_W_rel', 'L0_gnn_W_root', 'L0_gnn_bias', 'L0_gnn_W_res',
        'L0_gnn_b_res', 'L0_gnn_gamma', 'L0_gnn_beta']


def kernel(**inputs):
    import numpy as _np
    import concourse.bacc as _bacc
    from concourse import mybir as _mybir
    from concourse.bass_utils import run_bass_kernel_spmd as _run

    nc = _bacc.Bacc("TRN2", target_bir_lowering=False, num_devices=1)
    arrays, args = {}, []
    for name in _INS:
        a = _np.ascontiguousarray(inputs[name])
        arrays[f"in_{name}_dram"] = a
        args.append(nc.dram_tensor(f"in_{name}_dram", a.shape, _mybir.dt.from_np(a.dtype), kind="ExternalInput").ap())
    args.append(nc.dram_tensor("out_0_dram", inputs["x"].shape, _mybir.dt.float32, kind="ExternalOutput").ap())
    gnn(nc, *args)
    r = _run(nc, [arrays], core_ids=[0])
    return r.results[0]["out_0_dram"]
```

```python
from contextlib import ExitStack

import concourse.bass as bass
from concourse import mybir
import numpy as np

F32 = mybir.dt.float32
F32R = mybir.dt.float32r
BF16 = mybir.dt.bfloat16
I32 = mybir.dt.int32
ALU = mybir.AluOpType
ACT = mybir.ActivationFunctionType
AX = mybir.AxisListType

P = 128
CH = 16
WIN = 80
GE = P * CH
RPM = 4
EPS = 1e-5


def ceil_div(a, b):
    return -(-a // b)


def gnn(nc, x, src, dst, et, w_rel, w_root, bias, w_res, b_res, gamma, beta, out):
    N, F = x.shape
    E = src.shape[0]
    R = w_rel.shape[0]
    assert F == P and w_rel.shape[1] == P and w_rel.shape[2] == P
    NT = ceil_div(N, P)
    NLAST = N - (NT - 1) * P
    G = ceil_div(E, GE)
    ELAST = E - (G - 1) * GE
    PLAST = ELAST // CH
    assert ELAST % CH == 0 and G % 2 == 0 and NT % 2 == 1 and G > 6
    PASSES = ceil_div(N, WIN)
    NPIECE = R // RPM
    assert R == NPIECE * RPM + 1 and NPIECE % 4 == 0
    QC = NPIECE // 4 * RPM * F
    HC = max(N + WIN, NT * P)
    BG = 7
    NB = NT // BG
    assert NB * BG == NT and NB > 3
    BNC = 250
    assert N % BNC == 0

    ytab = nc.dram_tensor("ytab", (NT * P * R, F), F32, kind="Internal").ap()
    etpad = nc.dram_tensor("etpad", (G * GE,), BF16, kind="Internal").ap()
    ytab_tiles = ytab.rearrange("(t p r) f -> t p (r f)", p=P, r=R)
    etpad_rows = etpad.rearrange("(g e) -> g e", e=GE)

    with ExitStack() as ctx:
        def sb(name, shape, dt):
            return ctx.enter_context(nc.sbuf_tensor(name, shape, dt))

        def pb(name, shape, dt):
            return ctx.enter_context(nc.psum_tensor(name, shape, dt))

        def sem(name):
            return ctx.enter_context(nc.semaphore(name))

        w_hi = sb("w_hi", [P, R * F], F32R)
        w_lo = sb("w_lo", [P, R * F], F32R)
        stage = sb("stage", [P, R * F], F32)
        H = sb("H", [P, HC], F32)
        CT = sb("CT", [R, HC], F32)
        srcs = sb("srcs", [P, G * CH], I32)
        dsts = sb("dsts", [P, G * CH], I32)
        ets = sb("ets", [P, G * CH], I32)
        et16 = sb("et16", [P, G * CH], BF16)
        drow = sb("drow", [1, G], F32)
        basec = sb("basec", [P, G], F32)
        passb = sb("passb", [P, PASSES], F32)
        dloc2 = sb("dloc2", [P, 2, CH], F32)
        idx = [sb(f"idx{s}", [P, CH], I32) for s in range(2)]
        onehot_n = [sb(f"onehot_n{s}", [P, CH, WIN], BF16) for s in range(2)]
        onehot_r = [sb(f"onehot_r{s}", [P, CH, R], BF16) for s in range(2)]
        dcnt = sb("dcnt", [P, 2, CH], F32)
        rel1h = sb("rel1h", [R, 2, GE], BF16)
        wts = sb("wts", [P, 2, CH, WIN], F32)
        cf = sb("cf", [R, 4, WIN], F32)
        cinv = sb("cinv", [R, 2, 3, WIN], BF16)
        xt_in = sb("xt_in", [P, 2, F], F32)
        xT = [sb(f"xT{s}", [P, P], F32) for s in range(2)]
        x_hi = [sb(f"x_hi{s}", [P, P], F32R) for s in range(2)]
        x_lo = [sb(f"x_lo{s}", [P, P], F32R) for s in range(2)]
        wroot = sb("wroot", [P, F], F32)
        wres = sb("wres", [P, F], F32)
        ident = sb("ident", [P, P], F32)
        ones = sb("ones", [P, P], F32)
        iota_n = sb("iota_n", [P, WIN], F32)
        iota_r = sb("iota_r", [P, R], F32)
        pidx = sb("pidx", [P, 1], F32)
        cols = sb("cols", [P, 16], F32)
        flag = sb("flag", [1, 1], I32)
        bst = sb("bst", [P, N // BNC, 6], F32)
        etb = w_hi[0:R, 0:GE].bitcast(BF16).rearrange("r (s e) -> r s e", s=2)
        def raw_quarter(q, n):
            return (H[:, q * QC:q * QC + n] if q < 3 else
                    wts[:].rearrange("p s k w -> p (s k w)")[:, 0:n])
        ys = [stage[:, s * CH * F:(s + 1) * CH * F].rearrange("p (k f) -> p k f", f=F) for s in range(2)]
        xin = [stage[:, (2 * CH + s * BG) * F:(2 * CH + (s + 1) * BG) * F].rearrange("p (t f) -> p t f", f=F)
               for s in range(2)]
        oo = [stage[:, (2 * CH + (2 + s) * BG) * F:(2 * CH + (3 + s) * BG) * F].rearrange("p (t f) -> p t f", f=F)
              for s in range(2)]
        NS = 3
        lst = sb("lst", [P, NS, BG, 6], F32)
        lmv = sb("lmv", [P, NS, BG, 2], F32)
        lrs = sb("lrs", [P, NS, 4, BG], F32)
        (B_BIAS, B_RES, GAM, BET, BSUM, BAD, MV, STD, SCL, SHF) = (0, 1, 2, 3, 4, 5, 6, 8, 9, 10)
        LO, HI, TWO_ON, ONE_ON = 11, 12, 13, 14

        bank = [pb(f"bank{i}", [P, 512], F32) for i in range(4)]
        root_ps = pb("root_ps", [P, 512], F32)
        tr_ps = pb("tr_ps", [P, 512], F32)
        acc_ps = [pb(f"acc_ps{i}", [P, 512], F32) for i in range(2)]
        cnt_acc = [tr_ps[0:R, 0:WIN], root_ps[0:R, 0:WIN]]
        last_banks = [bank[0], bank[1], bank[2], bank[3], root_ps, tr_ps]

        loaded = {n: sem("loaded_" + n) for n in ("src", "dst", "et", "wroot", "small")}
        wrel_in = [sem(f"wrel_in{q}") for q in range(4)]
        padded = sem("padded")
        pads_in = sem("pads_in")
        consts = sem("consts")
        et16_done = sem("et16_done")
        etpad_in_dram = sem("etpad_in_dram")
        base_row = sem("base_row")
        base_ps = sem("base_ps")
        bad_rdy = sem("bad_rdy")
        bad_ps = sem("bad_ps")
        flag_rdy = sem("flag_rdy")
        dve_step = sem("dve_step")
        x_in = [sem(f"x_in{s}") for s in range(2)]
        xT_ps = sem("xT_ps")
        xT_rdy = sem("xT_rdy")
        piece_ps = sem("piece_ps")
        piece_out = sem("piece_out")
        root_done = sem("root_done")
        root_out = sem("root_out")
        w_hi_rdy = sem("w_hi_rdy")
        w_rdy = sem("w_rdy")
        x_hi_rdy = sem("x_hi_rdy")
        x_lo_rdy = sem("x_lo_rdy")
        tab_out = [sem(f"tab_out{q}") for q in range(4)]
        oh_rdy = sem("oh_rdy")
        cnt_ps = sem("cnt_ps")
        cnt_add = sem("cnt_add")
        cnt_step = sem("cnt_step")
        etb_in = [sem(f"etb_in{s}") for s in range(2)]
        idx_rdy = sem("idx_rdy")
        prep_step = sem("prep_step")
        rel_rdy = sem("rel_rdy")
        look_ps = sem("look_ps")
        wts_rdy = sem("wts_rdy")
        pool_turn = sem("pool_turn")
        sp_turn = sem("sp_turn")
        gathered = [sem(f"gathered{s}") for s in range(2)]
        msg_ps = sem("msg_ps")
        msg_add = sem("msg_add")
        norm_rdy = sem("norm_rdy")
        std_rdy = sem("std_rdy")
        relu_rdy = sem("relu_rdy")
        sum_ps = sem("sum_ps")
        row_step = sem("row_step")
        lv_rdy = sem("lv_rdy")
        lstd_rdy = sem("lstd_rdy")
        lnorm_rdy = sem("lnorm_rdy")
        o_rdy = sem("o_rdy")
        xr_in = [sem(f"xr_in{s}") for s in range(2)]
        o_out = [sem(f"o_out{s}") for s in range(2)]

        block = ctx.enter_context(nc.Block())

        def rows_ps(b, t):
            return last_banks[2 * (b % NS) + t // 4][:, t % 4 * P:(t % 4 + 1) * P]

        def col(c, n=1):
            return cols[:, c:c + n]

        def colvec(v):
            return v.rearrange("(p a) -> p a", a=1)

        def grp(t, g):
            return t[:, bass.ds(g * CH, CH)]

        def both_paths(eng, fast, general):
            eng.wait_ge(flag_rdy, 1)
            bad = eng.value_load(flag[0:1, 0:1], min_val=0, max_val=P)
            with eng.If(bad == 0):
                fast()
            with eng.Else():
                general()

        def general_passes(eng, one_pass, before_pass):
            with eng.Fori(0, PASSES) as p:
                one_pass(p)
                before_pass(p)

        @block.sync
        def _(sp):
            def load_x(i, s):
                sp.dma_start(xt_in[:, s, :], x[bass.ds(i * P, P), :]).then_inc(x_in[s], 16)

            load_x(0, 0)
            qr = QC // F
            for q in range(4):
                hi = (q + 1) * qr if q < 3 else R
                sp.dma_start(raw_quarter(q, (hi - q * qr) * F).rearrange("p (r f) -> p r f", f=F),
                             w_rel[q * qr:hi, :, :].rearrange("r p f -> p r f")).then_inc(wrel_in[q], 16)
            sp.dma_start(wroot[:], w_root).then_inc(loaded["wroot"], 16)
            sp.dma_start(wres[:], w_res).then_inc(loaded["wroot"], 16)
            for c, v in ((B_BIAS, bias), (B_RES, b_res), (GAM, gamma), (BET, beta)):
                sp.dma_start(col(c), colvec(v)).then_inc(loaded["small"], 16)
            load_x(1, 1)
            for n, t, v in (("et", ets, et), ("dst", dsts, dst), ("src", srcs, src)):
                full = v[0:(G - 1) * GE].rearrange("(g p k) -> p g k", p=P, k=CH)
                sp.dma_start(t[:, 0:(G - 1) * CH].rearrange("p (g k) -> p g k", k=CH), full).then_inc(loaded[n], 16)
                sp.wait_ge(padded, 2)
                sp.dma_start(t[0:PLAST, (G - 1) * CH:G * CH],
                             v[(G - 1) * GE:E].rearrange("(p k) -> p k", k=CH)).then_inc(loaded[n], 16)

            def store_tile(i):
                tile = ytab_tiles[bass.ds(i, 1), :, :].rearrange("t p c -> (t p) c")
                for q in range(4):
                    hi = (q + 1) * QC if q < 3 else R * F
                    sp.wait_ge(piece_out, i * NPIECE + (q + 1) * (NPIECE // 4))
                    if q == 3:
                        sp.wait_ge(root_out, i + 1)
                    sp.sem_inc(sp_turn)
                    sp.dma_start(tile[:, q * QC:hi], stage[:, q * QC:hi]).then_inc(tab_out[q], 16)

            with sp.Fori(0, (NT - 3) // 2) as j:
                for s in range(2):
                    i = 2 * j + s
                    sp.wait_ge(xT_ps, i + 1)
                    sp.sem_inc(sp_turn)
                    load_x(i + 2, s)
                    store_tile(i)
            for i in range(NT - 3, NT):
                if i == NT - 2:
                    sp.wait_ge(et16_done, 1)
                    sp.dma_start(etpad.rearrange("(g p k) -> p g k", p=P, k=CH),
                                 et16[:].rearrange("p (g k) -> p g k", k=CH)).then_inc(etpad_in_dram, 16)
                if i + 2 < NT:
                    sp.wait_ge(xT_ps, i + 1)
                if i + 2 < NT - 1:
                    load_x(i + 2, i % 2)
                elif i + 2 == NT - 1:
                    sp.wait_ge(padded, 3)
                    sp.dma_start(xt_in[0:NLAST, i % 2, :], x[(NT - 1) * P:N, :]).then_inc(x_in[i % 2], 16)
                store_tile(i)

            def rows(t, b, n):
                return t[bass.ds(b * BG * P, n * P), :].rearrange("(t p) f -> p t f", p=P)

            def load_res(b, s):
                if b == NB - 1:
                    sp.dma_start(xin[s][:, 0:BG - 1, :], rows(x, b, BG - 1)).then_inc(xr_in[s], 16)
                    sp.dma_start(xin[s][0:NLAST, BG - 1, :], x[(NT - 1) * P:N, :]).then_inc(xr_in[s], 16)
                else:
                    sp.dma_start(xin[s], rows(x, b, BG)).then_inc(xr_in[s], 16)

            for q in range(4):
                sp.wait_ge(tab_out[q], 16 * NT)
            load_res(0, 0)
            load_res(1, 1)

            sp.wait_ge(etpad_in_dram, 16)

            def load_etb(p, g, s, first):
                if not first:
                    sp.wait_ge(rel_rdy, p * G + g - 1)
                    sp.sem_inc(sp_turn)
                sp.dma_start(etb[:, s, :], etpad_rows[bass.ds(g, 1), :].to_broadcast([R, GE])).then_inc(etb_in[s], 16)

            def etb_pass(p):
                for s in range(2):
                    load_etb(p, s, s, True)
                with sp.Fori(1, G // 2) as j:
                    for s in range(2):
                        load_etb(p, 2 * j + s, s, False)

            def general_after(p):
                sp.wait_ge(msg_add, (p + 1) * G)
                sp.sem_inc(sp_turn)

            both_paths(sp, lambda: etb_pass(0), lambda: general_passes(sp, etb_pass, general_after))

            for b in range(NB):
                s = b % 2
                if b + 2 < NB:
                    sp.wait_ge(sum_ps, (b + 1) * BG)
                    load_res(b + 2, s)
                sp.wait_ge(o_rdy, b + 1)
                if b < NB - 1:
                    sp.dma_start(rows(out, b, BG), oo[s]).then_inc(o_out[s], 16)
                else:
                    sp.dma_start(rows(out, b, BG - 1), oo[s][:, 0:BG - 1, :]).then_inc(o_out[s], 16)
                    sp.dma_start(out[(NT - 1) * P:N, :], oo[s][0:NLAST, BG - 1, :]).then_inc(o_out[s], 16)
            sp.wait_ge(o_out[(NB - 1) % 2], 16 * ((NB + 1) // 2 + 1))
            sp.wait_ge(o_out[NB % 2], 16 * (NB // 2))

        @block.gpsimd
        def _(pool):
            nc.gpsimd.memset(ets[:, (G - 1) * CH:G * CH], -1).then_inc(padded, 1)
            nc.gpsimd.memset(srcs[:, (G - 1) * CH:G * CH], 1).then_inc(padded, 1)
            pool.dma_start(dsts[PLAST:P, (G - 1) * CH:G * CH],
                           dst[E - CH:E].rearrange("(a k) -> a k", a=1).to_broadcast([P - PLAST, CH])).then_inc(pads_in, 16)
            nc.gpsimd.memset(ones[:], 1.0).then_inc(consts, 1)
            pool.wait_ge(consts, 1)
            nc.gpsimd.affine_select(out=ident[:], in_=ones[:], compare_op=ALU.is_equal, fill=0.0, base=0,
                                    pattern=[[-1, P]], channel_multiplier=1).then_inc(consts, 1)
            nc.gpsimd.iota(iota_n[:], [[1, WIN]], base=0, channel_multiplier=0,
                           allow_small_or_imprecise_dtypes=True).then_inc(consts, 1)
            nc.gpsimd.iota(iota_r[:], [[1, R]], base=0, channel_multiplier=0,
                           allow_small_or_imprecise_dtypes=True).then_inc(consts, 1)
            nc.gpsimd.iota(pidx[:], [[1, 1]], base=0, channel_multiplier=1,
                           allow_small_or_imprecise_dtypes=True).then_inc(consts, 1)
            nc.gpsimd.iota(passb[:], [[WIN, PASSES]], base=0, channel_multiplier=0,
                           allow_small_or_imprecise_dtypes=True).then_inc(consts, 1)
            nc.gpsimd.memset(CT[:], 0.0).then_inc(consts, 1)
            nc.gpsimd.memset(H[:, NT * P:HC], 0.0).then_inc(consts, 1)
            pool.wait_ge(xT_ps, NT - 2)
            nc.gpsimd.memset(xt_in[:, (NT - 1) % 2, :], 0.0).then_inc(padded, 1)

            for q in range(4):
                pool.wait_ge(tab_out[q], 16 * NT)

            def gather(p, g, s, first):
                pool.wait_ge(idx_rdy, p * G + g + 1)
                if not first:
                    pool.wait_ge(msg_ps, p * G + g - 1)
                pool.sem_inc(pool_turn)
                for k in range(CH):
                    pool.indirect_dma_start(
                        out=ys[s][:, k, :], out_offset=None, in_=ytab,
                        in_offset=bass.IndirectOffsetOnAxis(ap=idx[s][:, k:k + 1], axis=0)).then_inc(gathered[s], 16)

            def gather_pass(p):
                for s in range(2):
                    gather(p, s, s, True)
                with pool.Fori(1, G // 2) as j:
                    for s in range(2):
                        gather(p, 2 * j + s, s, False)

            def general_after(p):
                pool.wait_ge(msg_add, (p + 1) * G)
                pool.sem_inc(pool_turn)

            both_paths(pool, lambda: gather_pass(0), lambda: general_passes(pool, gather_pass, general_after))

        @block.tensor
        def _(pe):
            def spread_bases():
                pe.wait_ge(base_row, 1)
                nc.tensor.matmul(acc_ps[0][:, 0:G], ones[0:1, :], drow[:], start=True, stop=True).then_inc(base_ps, 1)

            def sum_bad():
                pe.wait_ge(bad_rdy, 1)
                nc.tensor.matmul(acc_ps[0][0:1, G:G + 1], col(BAD), ones[:, 0:1], start=True, stop=True).then_inc(bad_ps, 1)

            def transpose_x(i, s, first, last):
                pe.wait_ge(x_in[s], 8 * (i - s) + 16)
                if not first:
                    pe.wait_ge(xT_rdy, i)
                nc.tensor.transpose(tr_ps[:, 0:P], xt_in[:, s, :], ident[:]).then_inc(xT_ps, 1)

            def table_tile(i, s, first, last):
                if not last:
                    transpose_x(i + 1, 1 - s, False, False)
                pe.wait_ge(x_hi_rdy, i + 1)
                pe.wait_ge(x_lo_rdy, i + 1)

                def product(out, lo, hi):
                    nc.tensor.matmul(out, x_hi[s][:], w_hi[:, lo:hi], start=True, stop=False)
                    nc.tensor.matmul(out, x_hi[s][:], w_lo[:, lo:hi], start=False, stop=False)
                    return nc.tensor.matmul(out, x_lo[s][:], w_hi[:, lo:hi], start=False, stop=True)

                for q in range(NPIECE):
                    if q % 2 == 0 and not (first and q < 4):
                        pe.wait_ge(piece_out, i * NPIECE + q - 2)
                    if first and q % 4 == 0:
                        pe.wait_ge(w_rdy, q // 4 + 1)
                    product(bank[q % 4][:], q * 512, (q + 1) * 512).then_inc(piece_ps, 1)
                    if q == 13:
                        if first:
                            pe.wait_ge(loaded["wroot"], 32)
                            pe.wait_ge(w_rdy, 4)
                        else:
                            pe.wait_ge(root_out, i)
                        product(root_ps[:, P:2 * P], NPIECE * 512, R * F)
                        nc.tensor.matmul(root_ps[:, 0:P], wroot[:], xT[s][:], start=True, stop=False)
                        nc.tensor.matmul(root_ps[:, 0:P], wres[:], xT[s][:], start=False,
                                         stop=True).then_inc(root_done, 1)

            def count_group(p, g, s, first2):
                pe.wait_ge(oh_rdy, p * G + g + 1)
                if not first2:
                    pe.wait_ge(cnt_add, p * G + g - 1)
                for k in range(CH):
                    ins = nc.tensor.matmul(cnt_acc[s], onehot_r[s][:, k, :], onehot_n[s][:, k, :],
                                           start=(k == 0), stop=(k == CH - 1))
                ins.then_inc(cnt_ps, 1)

            pe.wait_ge(consts, 2)
            transpose_x(0, 0, True, False)
            table_tile(0, 0, True, False)
            with pe.Fori(0, (NT - 5) // 2) as j:
                for u in (1, 2):
                    table_tile(2 * j + u, u % 2, False, False)
            spread_bases()
            table_tile(NT - 4, 1, False, False)
            table_tile(NT - 3, 0, False, False)
            sum_bad()
            table_tile(NT - 2, 1, False, False)
            table_tile(NT - 1, 0, False, True)
            pe.wait_ge(piece_out, NT * NPIECE)
            pe.wait_ge(root_out, NT)

            def count_pass(p):
                for g in range(2):
                    count_group(p, g, g, True)
                with pe.Fori(1, G // 2) as j:
                    for s in range(2):
                        count_group(p, 2 * j + s, s, False)

            def count_after(p):
                pe.wait_ge(cnt_add, (p + 1) * G)

            def lookup(p, g, s, first):
                pe.wait_ge(rel_rdy, p * G + g + 1)
                rel = rel1h[:, s, :].rearrange("r (p k) -> r k p", k=CH)
                for b in range(4):
                    if not first:
                        pe.wait_ge(wts_rdy, (p * G + g - 1) * CH + 4 * b + 4)
                    for k in range(4 * b, 4 * b + 4):
                        for part in range(3):
                            ins = nc.tensor.matmul(bank[b][:, (k - 4 * b) * WIN:(k - 4 * b + 1) * WIN],
                                                   rel[:, k, :], cinv[:, s, part, :],
                                                   start=(part == 0), stop=(part == 2))
                    ins.then_inc(look_ps, 1)

            def messages(p, g, s, first2):
                pe.wait_ge(gathered[s], (p * (G // 2) + (g - s) // 2 + 1) * 16 * CH if not isinstance(g, int)
                           else p * (G // 2) * 16 * CH + (g // 2 + 1) * 16 * CH)
                if not first2:
                    pe.wait_ge(msg_add, p * G + g - 1)
                for k in range(CH):
                    pe.wait_ge(wts_rdy, (p * G + g) * CH + k + 1)
                    ins = nc.tensor.matmul(acc_ps[s][:, 0:WIN], ys[s][:, k, :], wts[:, s, k, :],
                                           start=(k == 0), stop=(k == CH - 1))
                ins.then_inc(msg_ps, 1)

            def message_group(p, g, s, count):
                lookup(p, g, s, isinstance(g, int) and g == 0)
                if count:
                    count_group(p, g + 3, 1 - s, False)
                messages(p, g, s, isinstance(g, int) and g < 2)

            def message_pass(p, count):
                for g in range(3):
                    message_group(p, g, g % 2, count)
                with pe.Fori(0, (G - 6) // 2) as j:
                    for u in (3, 4):
                        message_group(p, 2 * j + u, u % 2, count)
                for g in range(G - 3, G):
                    message_group(p, g, g % 2, False)

            def general_after(p):
                pe.wait_ge(msg_add, (p + 1) * G)

            def fast():
                for g in range(3):
                    count_group(0, g, g % 2, g < 2)
                message_pass(0, True)

            def general():
                general_passes(pe, count_pass, count_after)
                general_passes(pe, lambda p: message_pass(p, False), general_after)

            both_paths(pe, fast, general)

            for b in range(NB):
                pe.wait_ge(relu_rdy, b + 1)
                pe.wait_ge(xr_in[b % 2], 16 * (b // 2 + 1) + (16 if b == NB - 1 else 0))
                if b >= NS:
                    pe.wait_ge(o_rdy, b - NS + 1)
                for t in range(BG):
                    i = b * BG + t
                    n = NLAST if i == NT - 1 else P
                    nc.tensor.matmul(rows_ps(b, t)[0:n, :], H[:, i * P:i * P + n], ident[:], start=True, stop=False)
                    nc.tensor.matmul(rows_ps(b, t)[0:n, :], ident[0:n, 0:n], xin[b % 2][0:n, t, :],
                                     start=False, stop=True).then_inc(sum_ps, 1)

        @block.scalar
        def _(act):
            def copy_x(i, s):
                act.wait_ge(xT_ps, i + 1)
                nc.scalar.activation(xT[s][:], tr_ps[:, 0:P], ACT.Copy).then_inc(xT_rdy, 1)
                act.wait_ge(xT_rdy, i + 1)
                nc.scalar.activation(x_hi[s][:], xT[s][:], ACT.Copy).then_inc(x_hi_rdy, 1)

            def tile(i, s, first, last):
                for q in range(NPIECE):
                    if q == NPIECE // 2 and not last:
                        copy_x(i + 1, 1 - s)
                    if not first and q % 4 == 0:
                        act.wait_ge(tab_out[q // 4], 16 * i)
                    if q % 2 == 0:
                        act.wait_ge(piece_ps, i * NPIECE + q + 2)
                    nc.scalar.activation(stage[:, q * 512:(q + 1) * 512], bank[q % 4][:],
                                         ACT.Copy).then_inc(piece_out, 1)
                act.wait_ge(root_done, i + 1)
                nc.scalar.activation(H[:, bass.ds(i * P, P)], root_ps[:, 0:P], ACT.Identity, bias=col(BSUM))
                nc.scalar.activation(stage[:, NPIECE * 512:], root_ps[:, P:2 * P],
                                     ACT.Copy).then_inc(root_out, 1)

            copy_x(0, 0)
            for q in range(4):
                n = QC if q < 3 else R * F - 3 * QC
                act.wait_ge(wrel_in[q], 16)
                nc.scalar.activation(w_hi[:, q * QC:q * QC + n], raw_quarter(q, n), ACT.Copy).then_inc(w_hi_rdy, 1)
            act.wait_ge(w_rdy, 4)
            act.wait_ge(dve_step, 1)
            tile(0, 0, True, False)
            with act.Fori(0, (NT - 3) // 2) as j:
                for u in (1, 2):
                    tile(2 * j + u, u % 2, False, False)
            tile(NT - 2, 1, False, False)
            tile(NT - 1, 0, False, True)

            act.wait_ge(norm_rdy, 1)
            nc.scalar.activation(col(STD), col(STD), ACT.Sqrt).then_inc(std_rdy, 1)
            act.wait_ge(norm_rdy, 2)

            def relu(b):
                h = H[:, b * BG * P:(b + 1) * BG * P]
                nc.scalar.activation(h, h, ACT.Relu, bias=col(SHF), scale=col(SCL)).then_inc(relu_rdy, 1)

            def root_of(b):
                act.wait_ge(lv_rdy, b + 1)
                nc.scalar.activation(lrs[:, b % NS, 1, :], lrs[:, b % NS, 0, :], ACT.Sqrt).then_inc(lstd_rdy, 1)

            def scale_rows(b):
                act.wait_ge(lnorm_rdy, b + 1)
                if b >= 2:
                    act.wait_ge(o_out[b % 2], 16 * (b // 2))
                for t in range(BG):
                    n = NLAST if b * BG + t == NT - 1 else P
                    ins = nc.scalar.activation(oo[b % 2][0:n, t, :], rows_ps(b, t)[0:n, :], ACT.Identity,
                                               bias=lrs[0:n, b % NS, 3, t:t + 1], scale=lrs[0:n, b % NS, 2, t:t + 1])
                ins.then_inc(o_rdy, 1)

            relu(0)
            relu(1)
            for b in range(NB):
                if b + 2 < NB:
                    relu(b + 2)
                root_of(b)
                if b >= 1:
                    scale_rows(b - 1)
            scale_rows(NB - 1)

        @block.vector
        def _(dve):
            def split_x(i, s):
                dve.wait_ge(x_hi_rdy, i + 1)
                nc.vector.tensor_tensor(x_lo[s][:], xT[s][:], x_hi[s][:], ALU.subtract).then_inc(x_lo_rdy, 1)

            split_x(0, 0)
            for q in range(4):
                n = QC if q < 3 else R * F - 3 * QC
                dve.wait_ge(w_hi_rdy, q + 1)
                nc.vector.tensor_tensor(w_lo[:, q * QC:q * QC + n], raw_quarter(q, n), w_hi[:, q * QC:q * QC + n],
                                        ALU.subtract).then_inc(w_rdy, 1)
            dve.wait_ge(loaded["small"], 64)
            nc.vector.tensor_tensor(col(BSUM), col(B_BIAS), col(B_RES), ALU.add).then_inc(dve_step, 1)

            with dve.Fori(0, (NT - 5) // 2) as j:
                for u in (1, 2):
                    split_x(2 * j + u, u % 2)
            split_x(NT - 4, 1)
            dve.wait_ge(loaded["et"], 32)
            nc.vector.tensor_copy(et16[:], ets[:]).then_inc(et16_done, 1)
            dve.wait_ge(loaded["dst"], 32)
            dve.wait_ge(loaded["src"], 32)
            dve.wait_ge(pads_in, 16)
            nc.vector.tensor_copy(drow[:], dsts[0:1, :].rearrange("p (g k) -> p g k", k=CH)[:, :, 0]
                                  ).then_inc(base_row, 1)
            dve.wait_ge(base_ps, 1)
            nc.vector.tensor_copy(basec[:], acc_ps[0][:, 0:G]).then_inc(dve_step, 1)
            dve.wait_ge(dve_step, 2)
            scratch = wts[:].rearrange("p s k w -> p (s k w)")
            d3 = dsts[:].rearrange("p (g k) -> p g k", k=CH)
            local, ahead, rise = scratch[:, 0:G * CH], scratch[:, 0:(G - 2) * CH], scratch[:, 0:G - 1]

            def bases_k(g0, n):
                return basec[:, g0:g0 + n].rearrange("p (g a) -> p g a", a=1).to_broadcast([P, n, CH])

            nc.vector.tensor_tensor(local.rearrange("p (g k) -> p g k", k=CH), d3, bases_k(0, G),
                                    ALU.subtract).then_inc(dve_step, 1)
            dve.wait_ge(dve_step, 3)
            nc.vector.tensor_reduce(col(HI), local, AX.X, ALU.max).then_inc(dve_step, 1)
            nc.vector.tensor_reduce(col(LO), local, AX.X, ALU.min).then_inc(dve_step, 1)
            dve.wait_ge(dve_step, 5)
            nc.vector.tensor_tensor(ahead.rearrange("p (g k) -> p g k", k=CH), d3[:, 0:G - 2, :],
                                    bases_k(2, G - 2), ALU.subtract).then_inc(dve_step, 1)
            dve.wait_ge(dve_step, 6)
            nc.vector.tensor_reduce(col(TWO_ON), ahead, AX.X, ALU.max).then_inc(dve_step, 1)
            dve.wait_ge(dve_step, 7)
            nc.vector.tensor_tensor(rise, basec[:, 1:G], basec[:, 0:G - 1], ALU.subtract).then_inc(dve_step, 1)
            dve.wait_ge(dve_step, 8)
            nc.vector.tensor_reduce(col(ONE_ON), rise, AX.X, ALU.min).then_inc(dve_step, 1)
            nc.vector.tensor_scalar(col(HI), col(HI), float(WIN - 1), None, ALU.is_gt).then_inc(dve_step, 1)
            nc.vector.tensor_scalar(col(TWO_ON), col(TWO_ON), 0.0, None, ALU.is_ge).then_inc(dve_step, 1)
            dve.wait_ge(dve_step, 11)
            nc.vector.scalar_tensor_tensor(out=col(HI), in0=col(LO), scalar=0.0, in1=col(HI), op0=ALU.is_lt,
                                           op1=ALU.max).then_inc(dve_step, 1)
            nc.vector.scalar_tensor_tensor(out=col(TWO_ON), in0=col(ONE_ON), scalar=0.0, in1=col(TWO_ON),
                                           op0=ALU.is_lt, op1=ALU.max).then_inc(dve_step, 1)
            dve.wait_ge(dve_step, 13)
            nc.vector.tensor_tensor(col(BAD), col(HI), col(TWO_ON), ALU.max).then_inc(bad_rdy, 1)
            split_x(NT - 3, 0)
            split_x(NT - 2, 1)
            dve.wait_ge(bad_ps, 1)
            nc.vector.tensor_copy(flag[:], acc_ps[0][0:1, G:G + 1]).then_inc(flag_rdy, 1)
            split_x(NT - 1, 0)
            dve.wait_ge(consts, 8)

            def bcast_k(t2, n):
                return t2.rearrange("p (k a) -> p k a", a=1).to_broadcast([t2.shape[0], CH, n])

            def bcast_n(t2, n):
                return t2.rearrange("p (a n) -> p a n", a=1).to_broadcast([t2.shape[0], CH, n])

            def local_dst(out, g, base_col):
                return nc.vector.tensor_tensor(out, grp(dsts, g), base_col.to_broadcast([P, CH]),
                                               ALU.subtract)

            def count_build(p, g, s, base_col, first2):
                n = (p * G + g) * 2
                if not first2:
                    dve.wait_ge(cnt_ps, p * G + g - 1)
                local_dst(dcnt[:, s, :], g, base_col).then_inc(cnt_step, 1)
                nc.vector.tensor_tensor(onehot_r[s][:], bcast_n(iota_r[:], R), bcast_k(grp(ets, g), R),
                                        ALU.is_equal).then_inc(cnt_step, 1)
                dve.wait_ge(cnt_step, n + 2)
                nc.vector.tensor_tensor(onehot_n[s][:], bcast_n(iota_n[:], WIN), bcast_k(dcnt[:, s, :], WIN),
                                        ALU.is_equal).then_inc(oh_rdy, 1)

            def count_sum(p, g, s, base, first):
                if not first:
                    dve.wait_ge(cnt_add, p * G + g)
                dve.wait_ge(cnt_ps, p * G + g + 1)
                w = CT[:, bass.ds(base, WIN)]
                nc.vector.tensor_tensor(w, w, cnt_acc[s], ALU.add).then_inc(cnt_add, 1)

            def fast_base(g):
                return dve.value_load(dsts[0:1, bass.ds(g * CH, 1)], min_val=0, max_val=N - 1)

            def fast_col(g):
                return basec[:, bass.ds(g, 1)]

            def count_pass(p, base_of, col_of):
                count_build(p, 0, 0, col_of(0), True)
                base = base_of(0)
                count_build(p, 1, 1, col_of(1), True)
                count_sum(p, 0, 0, base, True)
                with dve.Fori(0, (G - 2) // 2) as j:
                    for u in (1, 2):
                        g = 2 * j + u
                        base = base_of(g)
                        count_build(p, g + 1, (u + 1) % 2, col_of(g + 1), False)
                        count_sum(p, g, u % 2, base, False)
                base = base_of(G - 1)
                count_sum(p, G - 1, 1, base, False)

            def rows_to_gather(g, s):
                nc.vector.scalar_tensor_tensor(out=idx[s][:], in0=grp(srcs, g), scalar=float(R), in1=grp(ets, g),
                                               op0=ALU.mult, op1=ALU.add).then_inc(idx_rdy, 1)

            NPREP = 7

            def prepare(p, g, s, first2, base_of, col_of, counted):
                n = (p * G + g) * NPREP
                base = base_of(g)
                if not first2:
                    dve.wait_ge(msg_ps, p * G + g - 1)
                    rows_to_gather(g, s)
                local_dst(dloc2[:, s, :], g, col_of(g)).then_inc(prep_step, 1)
                dve.wait_ge(cnt_add, counted)
                nc.vector.tensor_scalar(cf[:, 0, :], CT[:, bass.ds(base, WIN)], 1.0, None,
                                        ALU.max).then_inc(prep_step, 1)
                dve.wait_ge(prep_step, n + 2)
                nc.vector.reciprocal(cf[:, 1, :], cf[:, 0, :]).then_inc(prep_step, 1)
                dve.wait_ge(prep_step, n + 3)
                nc.vector.tensor_copy(cinv[:, s, 0, :], cf[:, 1, :]).then_inc(prep_step, 1)
                dve.wait_ge(prep_step, n + 4)
                nc.vector.tensor_tensor(cf[:, 2, :], cf[:, 1, :], cinv[:, s, 0, :], ALU.subtract
                                        ).then_inc(prep_step, 1)
                dve.wait_ge(prep_step, n + 5)
                nc.vector.tensor_copy(cinv[:, s, 1, :], cf[:, 2, :]).then_inc(prep_step, 1)
                dve.wait_ge(prep_step, n + 6)
                nc.vector.tensor_tensor(cinv[:, s, 2, :], cf[:, 2, :], cinv[:, s, 1, :], ALU.subtract
                                        ).then_inc(prep_step, 1)
                if isinstance(g, int):
                    dve.wait_ge(etb_in[s], p * (G // 2) * 16 + (g // 2 + 1) * 16)
                else:
                    dve.wait_ge(etb_in[s], (p * (G // 2) + (g - s) // 2 + 1) * 16)
                dve.wait_ge(prep_step, n + 7)
                nc.vector.tensor_scalar(rel1h[:, s, :], etb[:, s, :], pidx[0:R, :], None,
                                        ALU.is_equal).then_inc(rel_rdy, 1)

            def weigh(p, g, s):
                for k in range(CH):
                    if k % 4 == 0:
                        dve.wait_ge(look_ps, (p * G + g) * 4 + k // 4 + 1)
                    nc.vector.scalar_tensor_tensor(
                        out=wts[:, s, k, :], in0=iota_n[:], scalar=dloc2[:, s, k:k + 1],
                        in1=bank[k // 4][:, (k % 4) * WIN:(k % 4 + 1) * WIN],
                        op0=ALU.is_equal, op1=ALU.mult).then_inc(wts_rdy, 1)

            def add_messages(p, g, s, base, first):
                if not first:
                    dve.wait_ge(msg_add, p * G + g)
                dve.wait_ge(msg_ps, p * G + g + 1)
                w = H[:, bass.ds(base, WIN)]
                nc.vector.tensor_tensor(w, w, acc_ps[s][:, 0:WIN], ALU.add).then_inc(msg_add, 1)

            def message_group(p, g, s, base_of, col_of, sum_ahead, build_ahead, counted):
                first = isinstance(g, int) and g == 0
                if sum_ahead:
                    count_sum(p, g + 2, s, base_of(g + 2), False)
                if build_ahead:
                    count_build(p, g + 3, 1 - s, col_of(g + 3), False)
                if counted is not None:
                    prepare(p, g + 1, 1 - s, first, base_of, col_of, counted)
                base = base_of(g)
                weigh(p, g, s)
                add_messages(p, g, s, base, first)

            def message_pass(p, base_of, col_of, count):
                def counted(g):
                    if not count:
                        return PASSES * G
                    return min(g + 2, G) if isinstance(g, int) else g + 2

                prepare(p, 0, 0, True, base_of, col_of, counted(0))
                for g in range(3):
                    message_group(p, g, g % 2, base_of, col_of, count, count, counted(g + 1))
                with dve.Fori(0, (G - 6) // 2) as j:
                    for u in (3, 4):
                        g = 2 * j + u
                        message_group(p, g, u % 2, base_of, col_of, count, count, counted(g + 1))
                for g in range(G - 3, G):
                    message_group(p, g, g % 2, base_of, col_of, count and g + 2 < G, False,
                                  counted(g + 1) if g + 1 < G else None)

            def fast():
                for g in range(2):
                    rows_to_gather(g, g)
                for g in range(3):
                    count_build(0, g, g % 2, fast_col(g), g < 2)
                    if g >= 1:
                        count_sum(0, g - 1, (g - 1) % 2, fast_base(g - 1), g == 1)
                dve.wait_ge(root_out, NT)
                message_pass(0, fast_base, fast_col, True)

            def general():
                def bases(p):
                    return lambda g: p * WIN, lambda g: passb[:, bass.ds(p, 1)]

                def one_pass(p):
                    for g in range(2):
                        rows_to_gather(g, g)
                    message_pass(p, *bases(p), False)

                general_passes(dve, lambda p: count_pass(p, *bases(p)), lambda p: dve.wait_ge(cnt_add, (p + 1) * G))
                dve.wait_ge(root_out, NT)
                general_passes(dve, one_pass, lambda p: dve.wait_ge(msg_add, (p + 1) * G))

            both_paths(dve, fast, general)
            dve.wait_ge(msg_add, G)

            k0 = 13
            for c in range(N // BNC):
                nc.vector.bn_stats(bst[:, c, :], H[:, c * BNC:(c + 1) * BNC]).then_inc(dve_step, 1)
            k0 += N // BNC
            dve.wait_ge(dve_step, k0)
            nc.vector.bn_aggr(col(MV, 2), bst[:].rearrange("p c s -> p (c s)")).then_inc(dve_step, 1)
            dve.wait_ge(dve_step, k0 + 1)
            nc.vector.tensor_scalar(col(STD), col(MV + 1), EPS, None, ALU.add).then_inc(norm_rdy, 1)
            dve.wait_ge(std_rdy, 1)
            nc.vector.reciprocal(col(SCL), col(STD)).then_inc(dve_step, 1)
            dve.wait_ge(dve_step, k0 + 2)
            nc.vector.tensor_tensor(col(SCL), col(SCL), col(GAM), ALU.mult).then_inc(dve_step, 1)
            dve.wait_ge(dve_step, k0 + 3)
            nc.vector.tensor_tensor(col(SHF), col(MV), col(SCL), ALU.mult).then_inc(dve_step, 1)
            dve.wait_ge(dve_step, k0 + 4)
            nc.vector.tensor_tensor(col(SHF), col(BET), col(SHF), ALU.subtract).then_inc(norm_rdy, 1)

            def row_stats(b):
                s = b % NS
                if b >= NS:
                    dve.wait_ge(o_rdy, b - NS + 1)
                for t in range(BG):
                    n = NLAST if b * BG + t == NT - 1 else P
                    if t % 4 == 0:
                        dve.wait_ge(sum_ps, b * BG + min(t + 4, BG))
                    nc.vector.bn_stats(lst[0:n, s, t, :], rows_ps(b, t)[0:n, :]).then_inc(row_step, 1)
                for t in range(BG):
                    n = NLAST if b * BG + t == NT - 1 else P
                    dve.wait_ge(row_step, step[0] + t + 1)
                    nc.vector.bn_aggr(lmv[0:n, s, t, :], lst[0:n, s, t, :]).then_inc(row_step, 1)
                step[0] += 2 * BG
                dve.wait_ge(row_step, step[0])
                nc.vector.tensor_scalar(lrs[:, s, 0, :], lmv[:, s, :, 1], EPS, None, ALU.add).then_inc(lv_rdy, 1)

            def row_scales(b):
                s = b % NS
                dve.wait_ge(lstd_rdy, b + 1)
                nc.vector.reciprocal(lrs[:, s, 2, :], lrs[:, s, 1, :]).then_inc(row_step, 1)
                step[0] += 1
                dve.wait_ge(row_step, step[0])
                nc.vector.scalar_tensor_tensor(out=lrs[:, s, 3, :], in0=lmv[:, s, :, 0], scalar=-1.0,
                                               in1=lrs[:, s, 2, :], op0=ALU.mult, op1=ALU.mult).then_inc(lnorm_rdy, 1)

            step = [0]
            row_stats(0)
            for b in range(1, NB):
                row_stats(b)
                row_scales(b - 1)
            row_scales(NB - 1)


_INS = ['x', 'src', 'dst', 'edge_type_65', 'L0_gnn_W_rel', 'L0_gnn_W_root', 'L0_gnn_bias', 'L0_gnn_W_res',
        'L0_gnn_b_res', 'L0_gnn_gamma', 'L0_gnn_beta']


def kernel(**inputs):
    import numpy as _np
    import concourse.bacc as _bacc
    from concourse import mybir as _mybir
    from concourse.bass_utils import run_bass_kernel_spmd as _run

    nc = _bacc.Bacc("TRN2", target_bir_lowering=False, num_devices=1)
    arrays, args = {}, []
    for name in _INS:
        a = _np.ascontiguousarray(inputs[name])
        arrays[f"in_{name}_dram"] = a
        args.append(nc.dram_tensor(f"in_{name}_dram", a.shape, _mybir.dt.from_np(a.dtype), kind="ExternalInput").ap())
    args.append(nc.dram_tensor("out_0_dram", inputs["x"].shape, _mybir.dt.float32, kind="ExternalOutput").ap())
    gnn(nc, *args)
    r = _run(nc, [arrays], core_ids=[0])
    return r.results[0]["out_0_dram"]
```
